# Optimizing a Trainium2 kernel written in Bass

```python
import numpy as np
import jax
import jax.numpy as jnp

def _softmax(x, axis=-1):
    return jax.nn.softmax(x, axis=axis)

def _gelu(x):
    return jax.nn.gelu(x, approximate=True)

def _silu(x):
    return jax.nn.silu(x)

def _sigmoid(x):
    return jax.nn.sigmoid(x)

def _layernorm(x, axis=-1, eps=1e-05):
    m = jnp.mean(x, axis=axis, keepdims=True)
    v = jnp.var(x, axis=axis, keepdims=True)
    return (x - m) / jnp.sqrt(v + eps)

def _scatter_add(tgt, idx, src, axis=0):
    return tgt.at[idx].add(src)

def _segment_sum(src, seg, n):
    return jax.ops.segment_sum(src, seg, n)
kernel_name = 'mk_gnn_preln_d1_gnn_r8_b86b4c'

def setup_inputs(seed: int=0):
    np.random.seed(seed)
    _w = jnp.asarray

    def _rec_inputs():
        import jax
        import jax.numpy as jnp
        _gk = jax.random.key(seed)
        x = -0.000202 + 1 * jax.random.normal(jax.random.fold_in(_gk, 1), (12500, 64), jnp.float32)
        src = jax.random.randint(jax.random.fold_in(_gk, 2), (400000,), 0, 12500, jnp.int32)
        dst = jax.random.randint(jax.random.fold_in(_gk, 3), (400000,), 0, 12500, jnp.int32)
        _o = jnp.argsort(dst, stable=True)
        src = src[_o]
        dst = dst[_o]
        return (x, src, dst)
    x, src, dst = _rec_inputs()

    def _L0_gnn_setup():
        import jax, jax.numpy as jnp
        import numpy as np
        N = 12500
        E = 150000
        D = 64
        L = 3
        key = jax.random.key(seed)
        ks = jax.random.split(key, 8)
        s = 1.0 / np.float32(np.sqrt(D))
        x = jax.random.normal(ks[0], (N, D), jnp.float32)
        edge_index = jax.random.randint(ks[1], (2, E), 0, N, dtype=jnp.int32)
        W1 = jax.random.normal(ks[2], (L, D, D), jnp.float32) * s
        b1 = jnp.zeros((L, D), jnp.float32)
        W2 = jax.random.normal(ks[3], (L, D, D), jnp.float32) * s
        b2 = jnp.zeros((L, D), jnp.float32)
        Wf = jax.random.normal(ks[4], (D, D), jnp.float32) * s
        bf = jnp.zeros((D,), jnp.float32)
        return {'x': x, 'edge_index': edge_index, 'W1': W1, 'b1': b1, 'W2': W2, 'b2': b2, 'Wf': Wf, 'bf': bf}
    _L0_gnn_all = _L0_gnn_setup()
    _L0_gnn_in = {k: v for k, v in _L0_gnn_all.items() if k in ('W1', 'b1', 'W2', 'b2', 'Wf', 'bf')}
    del _L0_gnn_all
    return {'x': x, 'src': src, 'dst': dst, 'L0_gnn_W1': _L0_gnn_in['W1'], 'L0_gnn_b1': _L0_gnn_in['b1'], 'L0_gnn_W2': _L0_gnn_in['W2'], 'L0_gnn_b2': _L0_gnn_in['b2'], 'L0_gnn_Wf': _L0_gnn_in['Wf'], 'L0_gnn_bf': _L0_gnn_in['bf']}

def reference(x, src, dst, L0_gnn_W1, L0_gnn_b1, L0_gnn_W2, L0_gnn_b2, L0_gnn_Wf, L0_gnn_bf):
    import jax
    import jax.numpy as jnp

    def _L0_gnn_ref(x, edge_index, W1, b1, W2, b2, Wf, bf):
        import jax, jax.numpy as jnp
        import numpy as np
        N = 12500
        E = 150000
        D = 64
        L = 3
        row, col = (edge_index[0], edge_index[1])
        h = x
        for l in range(L):

            def mlp(z):
                return jnp.maximum(z @ W1[l] + b1[l], 0.0) @ W2[l] + b2[l]
            msgs = mlp(h[col])
            agg = jax.ops.segment_sum(msgs, row, num_segments=N)
            h = mlp(h + agg)
        return h @ Wf + bf
    edge_index = jnp.stack([src, dst])
    h = jnp.maximum(_layernorm(x, axis=-1), 0.0)
    x = x + _L0_gnn_ref(h, edge_index, L0_gnn_W1, L0_gnn_b1, L0_gnn_W2, L0_gnn_b2, L0_gnn_Wf, L0_gnn_bf)
    return x

_drawn_inputs = setup_inputs


def setup_inputs(seed=0):
    import zlib

    import numpy as np

    out = dict(_drawn_inputs(seed))
    spreads = {'L0_gnn_b1': (0.0, 0.1), 'L0_gnn_b2': (0.0, 0.1), 'L0_gnn_bf': (0.0, 2.0)}
    factors = {'x': 119.276}
    for name, (base, spread) in spreads.items():
        noise = np.random.default_rng([zlib.crc32(name.encode()), seed]).standard_normal(out[name].shape)
        drawn = base * np.exp(spread * noise) if base else spread * noise
        out[name] = jnp.asarray(drawn.astype(out[name].dtype))
    for name, factor in factors.items():
        out[name] = (out[name] * factor).astype(out[name].dtype)
    return out
```

```python
from contextlib import ExitStack

import numpy as np
import concourse.bass as bass
from concourse import mybir
from concourse.alu_op_type import AluOpType as ALU

F32, F16, F8 = mybir.dt.float32, mybir.dt.float16, mybir.dt.float8e4
I32, U8 = mybir.dt.int32, mybir.dt.uint8
ACT = mybir.ActivationFunctionType
AX = mybir.AxisListType
ds = bass.ds

P = 128
N, D, L, E = 12500, 64, 3, 400000
KT = -(-N // P)
NP = KT * P
TAIL = N - (KT - 1) * P

GN = 4
HI = P // GN
LO = NP // HI
TG = P // GN
MAIN, OVER = 128, 64
WIN = MAIN + OVER
GRAN = 16
ROWS = E // GRAN
FAN = 32
TOP = -(-ROWS // FAN)
LAST_START = ROWS - WIN // GRAN
WT = -(-KT * TG // P)
KEYS = 2 * (TG + TG // 2)
COUNT_UNIT = 16.0
LO_BITS = 9
PK = 100
PC = E // PK
ROUND = 12582912.0
BIG = 1 << 24

PAIRS = TG // 2
HOTS = 8
PSLOTS = 3
BUILD = KT // 2
IPAIRS = 2 * PAIRS

NB = 448
SBB = 4
SBC = NB * SBB
SBT = SBC // P
SB = NP // SBC
CK = 7
CH = KT // CK
RING = 4
SLOT_LOADS = [len(range(s, CH, RING)) for s in range(RING)]
SPLIT = SB
EPS = 1e-5
LN_SUM_TO_MEAN = 1.0 / D


def gnn_kernel(nc, x, src, dst, W1, b1, W2, b2, Wf, bf, out):
    ctx = ExitStack()
    with ctx:
        def sb(name, shape, dt):
            return ctx.enter_context(nc.sbuf_tensor(name, shape, dt))

        def sem(name):
            return ctx.enter_context(nc.semaphore(name))

        def scratch(name, shape, dt):
            return nc.dram_tensor(name, shape, dt, kind="Internal").ap()

        counts_dram = scratch("counts_dram", (KT, TG, P, LO), U8)
        firsts_dram = scratch("firsts_dram", (TOP * FAN,), I32)
        packed_dram = scratch("packed_dram", (E,), I32)
        h0_dram = scratch("h0_dram", (NP, D), F32)
        h_dram = scratch("h_dram", (NP, D), F32)
        m_dram = scratch("m_dram", (NP, D), F32)
        agg_dram = scratch("agg_dram", (NP, D), F32)
        counts_rows = counts_dram.rearrange("k g p n -> (k g p n)").rearrange(
            "(c k r s) -> c r k s", k=CK, r=P, s=NP)

        hT = sb("hT", [P, NP], F32)
        msg = sb("msg", [P, KT, D], F32)
        parts = sb("parts", [P, KT, P], F16)
        W1s = sb("W1s", [P, L, D], F32)
        W2s = sb("W2s", [D, L, D], F32)
        Wfs = sb("Wfs", [D, D], F32)
        b1s = sb("b1s", [D, L], F32)
        b2s = sb("b2s", [D, L], F32)
        b2row = sb("b2row", [P, L, D], F32)
        bfrow = sb("bfrow", [P, D], F32)
        ident = sb("ident", [P, P], F32)
        ident16 = sb("ident16", [P, P], F16)
        ones = sb("ones", [P, P], F32)
        iota = sb("iota", [P, LO], F16)
        node_i = sb("node_i", [P, WT], I32)
        node = sb("node", [P, WT], F32)
        node_hi = sb("node_hi", [P, WT], F32)
        cnt = sb("cnt", [P, WT], F32)
        row = sb("row", [P, WT], F32)
        row_i = sb("row_i", [P, WT], I32)
        start_i = sb("start_i", [P, WT], I32)
        stat = sb("stat", [P, 4, KT], F32)
        peak = sb("peak", [P, BUILD], F32)
        scal = sb("scal", [P, L, 8], F32)
        finite = sb("finite", [P, SBB * SB], F32)
        good = sb("good", [P, 4], F32)
        good_i = sb("good_i", [1, 1], I32)
        pad_i = sb("pad_i", [1, TOP * FAN - ROWS], I32)

        ARENA = 95232
        arena = sb("arena", [P, ARENA], U8)

        def view(at, shape, dt, rows=P):
            size = {F32: 4, I32: 4, F16: 2, F8: 1}[dt]
            n = size * int(np.prod(shape))
            assert at % 4 == 0 and at + n <= ARENA
            v = arena[0:rows, at:at + n].bitcast(dt)
            if len(shape) == 2:
                v = v.rearrange("p (a b) -> p a b", a=shape[0])
            if len(shape) == 3:
                v = v.rearrange("p (a b c) -> p a b c", a=shape[0], b=shape[1])
            return v, at + n

        dst_t, at = view(0, [PC], I32, PK)
        src_t, at = view(at, [PC], I32, PK)
        pa, at = view(at, [PC], F32, PK)
        pb, at = view(at, [PC], F32, PK)
        pc, at = view(at, [PC], I32, PK)
        firsts, at = view(at, [ROWS // PK], I32, PK)
        first_i, at = view(at, [TOP], I32, 1)
        first_f, at = view(at, [TOP], F32, 1)
        keys, at = view(0, [4 * WT, KEYS], F16)
        win, end = view(at, [WT, WIN], I32)
        win_row, end = view(end, [WT, WIN], I32)
        win_rowf = win_row.bitcast(F32)
        fan, end = view(end, [WT, FAN], I32)
        fan_f, _ = view(at, [WT, FAN], F32)
        compare, _ = view(at, [TOP], F32)
        col_key, end = view(ARENA - 4 * WT * 2 * P, [WT, 2 * P], F16)
        row_key, end = view(end, [WT, 2 * P], F16)
        hot_c, at = view(at, [HOTS, 3, LO], F16)
        hot_r, at = view(at, [HOTS, 3, P], F16)
        stage, at = view(at, [2 * TG, LO], F8)
        assert at <= ARENA - 2 * WT * 2 * P
        key_now = sb("key_now", [P, 2, KEYS], F32)
        hS = sb("hS", [D, 2 * P], F32)
        uS = sb("uS", [D, 2 * P], F32)
        ring, at = view(0, [RING, CK * SBC], F8)
        zP, at = view(at, [SBC], F32)
        U, at = view(at, [SBC], F32, D)
        hN, at = view(at, [SBC], F32, D)
        V, at = view(at, [SBC], F32, D)
        x_t, at = view(at, [SBT, D], F32)
        out_t, at = view(at, [SBT, D], F32)
        tile_h, at = view(0, [D], F32)
        tile_agg, at = view(at, [D], F32)
        tile_x, at = view(at, [D], F32)
        tile_z, at = view(at, [D], F32)
        tile_hn, at = view(at, [D], F32)
        tile_m, at = view(at, [D], F32)
        zT_g, at = view(at, [P], F32, D)
        uT_g, at = view(at, [P], F32, D)
        hT_g, at = view(at, [P], F32, D)
        vT_g, at = view(at, [P], F32, D)
        e_dst, at = view(at, [1], I32)
        e_src, at = view(at, [1], I32)
        e_to, at = view(at, [1], I32)
        e_srcf, at = view(at, [1], F32)
        e_seen, at = view(at, [1], F32)
        e_msg, at = view(at, [D], F32)
        e_agg, at = view(at, [D], F32)
        e_diag, at = view(at, [P], F32)
        e_same, at = view(at, [P], F32)
        e_before, at = view(at, [P], F32)
        below, at = view(at, [P], F32)
        in_key, _ = view(0, [WT, WIN], F32)
        zero_zP = sb("zero_zP", [P, NB], F32)

        ps = ctx.enter_context(nc.psum_tensor("ps", [P, 8, 512], F32))

        s = {n: sem(n) for n in (
            "dst_loaded", "src_loaded", "x_loaded", "weights_loaded", "constants_made", "pad_made", "x_padded",
            "firsts_made", "firsts_stored", "tops_loaded", "tops_cast", "tops_spread",
            "packed_made", "packed_stored", "rows_found", "fans_gathered", "starts_found", "windows_gathered",
            "vector_chain", "variance_made", "root_made", "h0_made", "h0_stored", "h0_turned", "h0_kept", "h_zeroed",
            "keys_made", "keys_turned", "keys_kept", "keys_copied", "hots_made", "pair_multiplied", "pair_kept",
            "counts_stored_0", "counts_stored_1",
            "h_copied", "hidden0_done", "hidden0_kept", "message0_done", "message_kept",
            "peak_found", "finite_found", "peak_made", "peak_shared", "scale_made", "upper_made", "parts_made",
            "counts_used", "sums_done", "sums_read", "u_done", "u_kept", "h_done", "h_kept", "h_saved",
            "v_done", "v_kept", "m_done", "m_kept", "x_again", "out_done", "out_made", "out_read", "out_stored",
            "zeros_made", "good_made", "good_shared", "verdict",
        )}
        gs = {n: sem("general_" + n) for n in (
            "tensor", "scalar", "vector", "loaded", "stored", "zeros_made", "agg_cleared", "below_made")}
        es = [{n: sem(f"edges_{n}_{l}") for n in (
            "dst_loaded", "src_loaded", "messages", "sums", "vector", "tensor", "added")} for l in range(L)]
        counts_loaded = [sem(f"counts_loaded_{r}") for r in range(RING)]
        counts_stored = [s["counts_stored_0"], s["counts_stored_1"]]

        chain = [0]

        def link(ins, eng):
            chain[0] += 1
            ins.then_inc(s["vector_chain"], 1)
            eng.wait_ge(s["vector_chain"], chain[0])

        passed = {e: sem(f"waits_passed_{e}") for e in ("sync", "scalar", "tensor", "gpsimd")}


        def wait_alone(eng, semaphore, value):
            eng.wait_ge(semaphore, value)
            if not isinstance(value, int):
                eng.sem_inc(passed[{"SP": "sync", "Activation": "scalar", "PE": "tensor", "Pool": "gpsimd"}[eng.engine.name]], 1)

        TILE_SIGNALS = {"tensor": [3] + [6] * (L - 1) + [4], "scalar": [2] + [4] * (L - 1) + [3],
                        "vector": [2] + [3] * (L - 1) + [3], "loaded": [16] + [32] * (L - 1) + [48],
                        "stored": [16] + [32] * (L - 1) + [16]}
        EDGE_CHUNKS = E // P

        def tiles_before(kind, l, t):
            each = TILE_SIGNALS[kind]
            return t * each[l + 1] + KT * sum(each[:l + 1])

        def general(eng, tile, edges):
            eng.wait_ge(s["verdict"], 2)
            fine = eng.value_load(good_i[0:1, 0:1], min_val=0, max_val=1)
            with eng.If(fine < 1):
                for l in range(-1, L):
                    if tile is not None:
                        with eng.Fori(0, KT - 1) as i:
                            tile(l, i)
                        tile(l, KT - 1)
                    if edges is not None and l < L - 1:
                        edges(l + 1)

        block = ctx.enter_context(nc.Block())

        @block.sync
        def _(sp):
            sp.dma_start(dst_t, dst.rearrange("(p c) -> p c", p=PK)).then_inc(s["dst_loaded"], 16)
            sp.dma_start(src_t, src.rearrange("(p c) -> p c", p=PK)).then_inc(s["src_loaded"], 16)
            weights = [(W1s[0:D], W1.rearrange("l k m -> k l m")), (W1s[D:P], W1.rearrange("l k m -> k l m")),
                       (W2s[:], W2.rearrange("l k m -> k l m")), (Wfs[:], Wf), (b1s[:], b1.rearrange("l d -> d l")),
                       (b2s[:], b2.rearrange("l d -> d l")),
                       (b2row[:], b2.rearrange("l d -> (l d)").partition_broadcast(P)), (bfrow[:], bf.partition_broadcast(P))]
            for to, frm in weights:
                if to.ndim == 3 and to.shape[0] == P and frm.ndim == 2:
                    to = to.rearrange("p l d -> p (l d)")
                with nc.allow_non_contiguous_dma(reason="192 biases"):
                    sp.dma_start(to, frm).then_inc(s["weights_loaded"], 16)
            sp.wait_ge(s["firsts_made"], 1)
            sp.wait_ge(s["pad_made"], 1)
            sp.dma_start(firsts_dram[0:ROWS].rearrange("(p c) -> p c", p=PK), firsts).then_inc(s["firsts_stored"], 16)
            sp.dma_start(firsts_dram[ROWS:].rearrange("(p c) -> p c", p=1), pad_i[:]).then_inc(s["firsts_stored"], 16)
            sp.wait_ge(s["firsts_stored"], 32)
            with nc.allow_non_contiguous_dma(reason="one number of each row"):
                sp.dma_start(first_i, firsts_dram.rearrange("(p r f) -> p r f", p=1, f=FAN)[:, :, 0]).then_inc(
                    s["tops_loaded"], 16)
            sp.wait_ge(s["packed_made"], 1)
            sp.dma_start(packed_dram.rearrange("(p c) -> p c", p=PK), pc).then_inc(s["packed_stored"], 16)
            sp.wait_ge(s["h0_made"], 1)
            sp.dma_start(h0_dram.rearrange("(k p) d -> p k d", p=P), msg[:]).then_inc(s["h0_stored"], 16)

            with sp.Fori(0, BUILD) as i:
                for u in range(2):
                    wait_alone(sp, s["pair_kept"], i * IPAIRS + (u + 1) * PAIRS)
                    sp.dma_start(counts_dram[ds(i * 2 + u, 1)].rearrange("k g p n -> p (k g) n"),
                                 stage[:, u * TG:(u + 1) * TG, :].bitcast(U8)).then_inc(counts_stored[u], 16)

            sp.wait_ge(counts_stored[0], 16 * BUILD)
            sp.wait_ge(counts_stored[1], 16 * BUILD)
            sp.wait_ge(s["verdict"], 1)

            def load_stretch(sbase, l, first):
                g = sbase + l * SB
                for c in range(CH):
                    r = c % RING
                    if c >= RING:
                        wait_alone(sp, s["counts_used"], g * (CH - 1) + (c - RING + 1))
                    elif not first:
                        before = max(k for k in range(CH) if k % RING == r)
                        if before == CH - 1:
                            wait_alone(sp, s["sums_done"], g * SBB)
                        else:
                            wait_alone(sp, s["counts_used"], g * (CH - 1) + (before + 1 - (CH - 1)))
                    sp.dma_start(ring[:, r, :].rearrange("p (k n) -> p k n", k=CK).bitcast(U8),
                                 counts_rows[c][:, :, ds(sbase * SBC, SBC)]).then_inc(counts_loaded[r], 16)

            def load_x(sbase):
                sp.dma_start(x_t, x[ds((sbase - 1) * SBC, SBC), :].rearrange("(k p) d -> p k d", p=P)).then_inc(
                    s["x_again"], 16)

            for l in range(L):
                load_stretch(0, l, l == 0)
                with sp.Fori(1, SB) as i:
                    if l == L - 1:
                        load_x(i)
                    load_stretch(i, l, False)
                    if l == L - 1:
                        wait_alone(sp, s["out_made"], 2 * i)
                        sp.dma_start(out[ds((i - 1) * SBC, SBC), :].rearrange("(k p) d -> p k d", p=P), out_t).then_inc(
                            s["out_stored"], 16)
            sp.wait_ge(s["out_made"], 2 * (SB - 1))
            last = (SB - 1) * SBC
            sp.dma_start(x_t[:, 0:SBT - 1, :], x[last:last + (SBT - 1) * P, :].rearrange("(k p) d -> p k d", p=P)).then_inc(
                s["x_again"], 16)
            sp.dma_start(x_t[0:TAIL, SBT - 1, :], x[last + (SBT - 1) * P:N, :]).then_inc(s["x_again"], 16)
            sp.wait_ge(s["out_made"], 2 * SB)
            sp.dma_start(out[last:last + (SBT - 1) * P, :].rearrange("(k p) d -> p k d", p=P),
                         out_t[:, 0:SBT - 1, :]).then_inc(s["out_stored"], 16)
            sp.dma_start(out[last + (SBT - 1) * P:N, :], out_t[0:TAIL, SBT - 1, :]).then_inc(s["out_stored"], 16)
            sp.wait_ge(s["out_stored"], 16 * (SB + 1))
            sp.wait_ge(s["h0_stored"], 16)

            def tile(l, i):
                rows = ds(i * P, P)
                n = TAIL if isinstance(i, int) else P
                sp.dma_start(tile_h, (h0_dram if l <= 0 else h_dram)[rows, :]).then_inc(gs["loaded"], 16)
                if l >= 0:
                    sp.dma_start(tile_agg, agg_dram[rows, :]).then_inc(gs["loaded"], 16)
                if l == L - 1:
                    sp.dma_start(tile_x[0:n], x[ds(i * P, n), :]).then_inc(gs["loaded"], 16)
                before = tiles_before("vector", l, i)
                if 0 <= l < L - 1:
                    wait_alone(sp, gs["vector"], before + 2)
                    sp.dma_start(h_dram[rows, :], tile_hn).then_inc(gs["stored"], 16)
                wait_alone(sp, gs["vector"], before + TILE_SIGNALS["vector"][l + 1])
                if l < L - 1:
                    sp.dma_start(m_dram[rows, :], tile_m).then_inc(gs["stored"], 16)
                else:
                    sp.dma_start(out[ds(i * P, n), :], tile_m[0:n]).then_inc(gs["stored"], 16)
                wait_alone(sp, gs["stored"], tiles_before("stored", l, i) + TILE_SIGNALS["stored"][l + 1])

            def edges(l):
                sp.wait_ge(gs["stored"], tiles_before("stored", l, 0))
                sp.wait_ge(gs["zeros_made"], 1)
                sp.dma_start(agg_dram.rearrange("(k p) d -> p k d", p=P), msg[:]).then_inc(gs["agg_cleared"], 16)
                sp.wait_ge(gs["agg_cleared"], 16 * (l + 1))
                with sp.Fori(0, EDGE_CHUNKS) as c:
                    sp.dma_start(e_dst, dst[ds(c * P, P)].unsqueeze(1)).then_inc(es[l]["dst_loaded"], 16)
                    sp.dma_start(e_src, src[ds(c * P, P)].unsqueeze(1)).then_inc(es[l]["src_loaded"], 16)
                    wait_alone(sp, es[l]["added"], c * 16 + 16)

            general(sp, tile, edges)

        @block.gpsimd
        def _(pool):
            nc.gpsimd.memset(msg[:, KT - 1, :], 0.0).then_inc(s["x_padded"], 1)
            pool.wait_ge(s["x_padded"], 1)
            pool.dma_start(msg[:, 0:KT - 1, :], x[0:(KT - 1) * P, :].rearrange("(k p) d -> p k d", p=P)).then_inc(
                s["x_loaded"], 16)
            pool.dma_start(msg[0:TAIL, KT - 1, :], x[(KT - 1) * P:N, :]).then_inc(s["x_loaded"], 16)
            nc.gpsimd.memset(pad_i[:], BIG).then_inc(s["pad_made"], 1)
            nc.gpsimd.memset(ones[:], 1.0).then_inc(s["constants_made"], 1)
            nc.gpsimd.iota(iota[:], pattern=[[1, LO]], base=0, channel_multiplier=0,
                           allow_small_or_imprecise_dtypes=True).then_inc(s["constants_made"], 1)
            nc.gpsimd.iota(node_i[:], pattern=[[GN * P, WT]], base=0, channel_multiplier=GN).then_inc(
                s["constants_made"], 1)
            pool.wait_ge(s["constants_made"], 3)
            nc.gpsimd.affine_select(out=ident[:], in_=ones[:], compare_op=ALU.is_equal, fill=0.0, base=0,
                                    pattern=[[-1, P]], channel_multiplier=1).then_inc(s["constants_made"], 1)
            pool.wait_ge(s["constants_made"], 4)
            nc.gpsimd.tensor_copy(ident16[:], ident[:]).then_inc(s["constants_made"], 1)
            pool.wait_ge(s["constants_made"], 5)
            nc.gpsimd.memset(hT[D:P, :], 0.0).then_inc(s["h_zeroed"], 1)
            pool.wait_ge(s["h_zeroed"], 1)

            pool.wait_ge(s["rows_found"], 1)
            pool.wait_ge(s["firsts_stored"], 32)
            for t in range(WT):
                pool.indirect_dma_start(fan[:, t, :], None, firsts_dram.rearrange("(r f) -> r f", f=FAN),
                                        bass.IndirectOffsetOnAxis(ap=row_i[:, t:t + 1], axis=0)).then_inc(
                    s["fans_gathered"], 16)
            pool.wait_ge(s["starts_found"], 1)
            pool.wait_ge(s["packed_stored"], 16)
            for t in range(WT):
                pool.indirect_dma_start(win[:, t, :], None, packed_dram.rearrange("(r f) -> r f", f=GRAN),
                                        bass.IndirectOffsetOnAxis(ap=start_i[:, t:t + 1], axis=0)).then_inc(
                    s["windows_gathered"], 16)

            pool.wait_ge(s["h0_kept"], -(-KT // 4))

            def copy_h(i, first):
                if not first:
                    pool.wait_ge(s["hidden0_done"], i)
                nc.gpsimd.tensor_copy(hS[:], hT[0:D, ds(i * 2 * P, 2 * P)]).then_inc(s["h_copied"], 1)

            copy_h(0, True)
            with pool.Fori(1, BUILD) as i:
                copy_h(i, False)

            for l in range(L):
                pool.wait_ge(s["peak_made"], l + 1)
                nc.gpsimd.partition_all_reduce(scal[:, l, 1:2], scal[:, l, 0:1], P, bass.bass_isa.ReduceOp.max).then_inc(
                    s["peak_shared"], 1)
                if l == L - 1:
                    break
                with pool.Fori(0, SB) as i:
                    pool.wait_ge(s["h_kept"], (i + l * SB) * SBB + SBB)
                    nc.gpsimd.tensor_copy(hT[0:D, ds(i * SBC, SBC)], hN).then_inc(s["h_saved"], 1)
            pool.wait_ge(s["good_made"], 1)
            nc.gpsimd.partition_all_reduce(good[:, 2:4], good[:, 0:2], P, bass.bass_isa.ReduceOp.add).then_inc(
                s["good_shared"], 1)

            def edges(l):
                if l == 0:
                    nc.gpsimd.affine_select(out=below, in_=ones[:], compare_op=ALU.is_gt, fill=0.0, base=0,
                                            pattern=[[-1, P]], channel_multiplier=1).then_inc(gs["below_made"], 1)
                with pool.Fori(0, EDGE_CHUNKS) as c:
                    wait_alone(pool, es[l]["dst_loaded"], c * 16 + 16)
                    pool.indirect_dma_start(e_msg, None, m_dram, bass.IndirectOffsetOnAxis(ap=e_dst, axis=0)).then_inc(
                        es[l]["messages"], 16)
                    wait_alone(pool, es[l]["src_loaded"], c * 16 + 16)
                    pool.indirect_dma_start(e_agg, None, agg_dram, bass.IndirectOffsetOnAxis(ap=e_src, axis=0)).then_inc(
                        es[l]["sums"], 16)
                    wait_alone(pool, es[l]["vector"], c * 7 + 7)
                    pool.indirect_dma_start(agg_dram, bass.IndirectOffsetOnAxis(ap=e_to, axis=0), e_agg, None,
                                            bounds_check=NP - 1, oob_is_err=False).then_inc(es[l]["added"], 16)

            general(pool, None, edges)

        @block.vector
        def _(dve):
            v = nc.vector
            dve.wait_ge(s["dst_loaded"], 16)
            v.tensor_copy(firsts, dst_t.rearrange("p (c g) -> p c g", g=GRAN)[:, :, 0]).then_inc(s["firsts_made"], 1)
            dve.wait_ge(s["src_loaded"], 16)
            link(v.tensor_scalar(pa, src_t, 1.0 / LO, -0.5 + 1.0 / 1024, ALU.mult, ALU.add), dve)
            link(v.tensor_scalar(pb, pa, ROUND, ROUND, ALU.add, ALU.subtract), dve)
            link(v.scalar_tensor_tensor(pc, pb, -float(LO), src_t, ALU.mult, ALU.add), dve)
            link(v.scalar_tensor_tensor(src_t, dst_t, float(HI), pb, ALU.mult, ALU.add), dve)
            v.tensor_scalar(dst_t, src_t, LO_BITS, None, ALU.logical_shift_left).then_inc(s["vector_chain"], 1)
            chain[0] += 1
            dve.wait_ge(s["vector_chain"], chain[0])
            v.tensor_tensor(pc, dst_t, pc, ALU.bitwise_or).then_inc(s["packed_made"], 1)

            dve.wait_ge(s["constants_made"], 3)
            link(v.tensor_copy(node[:], node_i[:]), dve)
            link(v.tensor_scalar(node_hi[:], node[:], float(HI), None, ALU.mult), dve)
            dve.wait_ge(s["tops_loaded"], 16)
            v.tensor_copy(first_f, first_i).then_inc(s["tops_cast"], 1)
            dve.wait_ge(s["tops_spread"], 1)
            dve.wait_ge(s["packed_stored"], 16)
            half = TOP // 2
            tops = ps[:, 0:2, 0:half]
            comp = compare.rearrange("p (a b) -> p a b", a=2)
            for t in range(WT):
                link(v.tensor_scalar(comp, tops, node[:, t:t + 1], None, ALU.is_lt), dve)
                link(v.tensor_reduce(cnt[:, t:t + 1], comp, AX.XY, ALU.add), dve)
            link(v.tensor_scalar(row[:], cnt[:], -1.0, 0.0, ALU.add, ALU.max), dve)
            v.tensor_copy(row_i[:], row[:]).then_inc(s["rows_found"], 1)

            dve.wait_ge(s["x_loaded"], 32)
            sq = parts[:].rearrange("p k c -> p (k c)").bitcast(F32).rearrange("p (k d) -> p k d", d=D)
            mean, var, inv, tmp = (stat[:, j, :] for j in range(4))

            def wide(a):
                return a.unsqueeze(2).to_broadcast([P, KT, D])

            link(v.tensor_reduce(mean, msg[:], AX.X, ALU.add), dve)
            link(v.tensor_scalar(mean, mean, LN_SUM_TO_MEAN, None, ALU.mult), dve)
            link(v.tensor_tensor(msg[:], msg[:], wide(mean), ALU.subtract), dve)
            link(v.tensor_tensor(sq, msg[:], msg[:], ALU.mult), dve)
            link(v.tensor_reduce(var, sq, AX.X, ALU.add), dve)
            v.tensor_scalar(var, var, LN_SUM_TO_MEAN, EPS, ALU.mult, ALU.add).then_inc(s["variance_made"], 1)
            dve.wait_ge(s["root_made"], 1)
            link(v.reciprocal(inv, inv), dve)
            link(v.tensor_tensor(tmp, inv, inv, ALU.mult), dve)
            link(v.tensor_tensor(tmp, tmp, var, ALU.mult), dve)
            link(v.tensor_scalar(tmp, tmp, -0.5, 1.5, ALU.mult, ALU.add), dve)
            link(v.tensor_tensor(inv, inv, tmp, ALU.mult), dve)
            v.scalar_tensor_tensor(msg[:], msg[:], 0.0, wide(inv), ALU.max, ALU.mult).then_inc(s["h0_made"], 1)

            dve.wait_ge(s["fans_gathered"], 16 * WT)
            nodes = node[:].unsqueeze(2).to_broadcast([P, WT, FAN])
            link(v.tensor_tensor(fan_f, fan, nodes, ALU.is_lt), dve)
            link(v.tensor_reduce(cnt[:], fan_f, AX.X, ALU.add), dve)
            link(v.tensor_scalar(cnt[:], cnt[:], -1.0, 0.0, ALU.add, ALU.max), dve)
            link(v.scalar_tensor_tensor(row[:], row[:], float(FAN), cnt[:], ALU.mult, ALU.add), dve)
            v.tensor_scalar(start_i[:], row[:], float(LAST_START), None, ALU.min).then_inc(s["starts_found"], 1)

            dve.wait_ge(s["windows_gathered"], 16 * WT)
            link(v.tensor_scalar(win_row, win, LO_BITS, None, ALU.arith_shift_right), dve)
            link(v.tensor_scalar(win, win, (1 << LO_BITS) - 1, None, ALU.bitwise_and), dve)
            link(v.tensor_tensor(win_rowf, win_row, node_hi[:].unsqueeze(2).to_broadcast([P, WT, WIN]),
                                 ALU.subtract), dve)
            link(v.tensor_scalar(row_key[:, :, 0:WIN], win_rowf, float(P), -1.0, ALU.min, ALU.max), dve)
            link(v.tensor_copy(col_key[:, :, 0:WIN], win), dve)
            link(v.tensor_copy(row_key[:, :, WIN:2 * P], row_key[:, :, MAIN:WIN]), dve)
            v.tensor_copy(col_key[:, :, WIN:2 * P], col_key[:, :, MAIN:WIN]).then_inc(s["keys_made"], 1)

            for t in range(WT):
                dve.wait_ge(s["keys_turned"], t + 1)
                bank = ps[:, 4 + t % 4, :].bitcast(F16).rearrange("p (a g) -> p a g", a=8)
                to = keys[:, 4 * t:4 * t + 4, :]
                for j in range(2):
                    base = j * (TG + TG // 2)
                    v.tensor_copy(to[:, :, base:base + TG],
                                  bank[:, 2 * j, :].rearrange("p (k g) -> p k g", k=4))
                    over = bank[:, 2 * j + 1, :].rearrange("p (k g two) -> p k g two", k=4, two=2)
                    v.tensor_copy(to[0:OVER, :, base + TG:base + TG + TG // 2], over[0:OVER, :, :, 0])
                    last = v.tensor_copy(to[OVER:P, :, base + TG:base + TG + TG // 2], over[OVER:P, :, :, 1])
                last.then_inc(s["keys_kept"], 1)
            dve.wait_ge(s["keys_kept"], WT)

            def hot_tile(i, first):
                for q in range(IPAIRS):
                    u, j, slot = q // PAIRS, q % PAIRS, q % HOTS
                    if j == 0:
                        v.tensor_copy(key_now[:, u, :], keys[:, ds(i * 2 + u, 1), :].rearrange("p a k -> p (a k)")).then_inc(
                            s["keys_copied"], 1)
                        dve.wait_ge(s["keys_copied"], i * 2 + u + 1)
                    if not first or q >= HOTS:
                        dve.wait_ge(s["pair_multiplied"], i * IPAIRS + q - HOTS + 1)
                    rows = [2 * j, 2 * j + 1, TG + j]
                    for n, k in enumerate(rows):
                        v.tensor_scalar(hot_r[:, slot, n, :], iota[:, 0:P], key_now[:, u, k:k + 1], None, ALU.is_equal)
                        k += KEYS // 2
                        last = v.tensor_scalar(hot_c[:, slot, n, :], iota[:], key_now[:, u, k:k + 1], None,
                                               ALU.is_equal)
                    last.then_inc(s["hots_made"], 1)
                    if q == 16:
                        dve.wait_ge(s["message0_done"], i + 1)
                        v.tensor_tensor(msg[:, ds(i * 2, 2), :], ps[:, 7, 0:2 * D].rearrange("p (k d) -> p k d", k=2),
                                        b2row[:, 0:1, :].to_broadcast([P, 2, D]), ALU.add).then_inc(s["message_kept"], 1)
                    if q == 18:
                        dve.wait_ge(s["message_kept"], i + 1)
                        v.tensor_reduce(peak[:, ds(i, 1)], msg[:, ds(i * 2, 2), :].rearrange("p k d -> p (k d)"), AX.X,
                                        ALU.max, apply_absolute_value=True).then_inc(s["peak_found"], 1)

            dve.wait_ge(s["h0_stored"], 16)
            hot_tile(0, True)
            with dve.Fori(1, BUILD) as i:
                hot_tile(i, False)

            dve.wait_ge(counts_stored[0], 16 * BUILD)
            dve.wait_ge(counts_stored[1], 16 * BUILD)
            link(v.tensor_scalar(in_key, row_key[:, :, 0:WIN], 0.0, None, ALU.is_ge), dve)
            link(v.scalar_tensor_tensor(in_key, row_key[:, :, 0:WIN], P - 1.0, in_key, ALU.is_le, ALU.mult), dve)
            v.tensor_reduce(good[:, 0:1], in_key, AX.XY, ALU.add).then_inc(s["verdict"], 1)

            def scale_and_split(l, peaks):
                c = [scal[:, l, j:j + 1] for j in range(8)]
                dve.wait_ge(s["peak_found"], BUILD + l * 2 * SB)
                v.tensor_reduce(c[0], peak[:, 0:peaks], AX.X, ALU.max).then_inc(s["peak_made"], 1)
                dve.wait_ge(s["peak_shared"], l + 1)
                link(v.tensor_scalar(c[2], c[1], 2.0 ** -100, None, ALU.max), dve)
                link(v.tensor_scalar(c[3].bitcast(I32), c[2].bitcast(I32), 0x7F800000, None, ALU.bitwise_and), dve)
                link(v.reciprocal(c[4], c[3]), dve)
                link(v.tensor_scalar(c[6], c[3], 2.0 ** -14 / COUNT_UNIT, None, ALU.mult), dve)
                v.tensor_scalar(c[5], c[4], 2.0 ** 14, None, ALU.mult).then_inc(s["scale_made"], 1)
                for n in range(SPLIT):
                    t = slice(n * SBT, (n + 1) * SBT)
                    dve.wait_ge(s["upper_made"], l * SPLIT + n + 1)
                    v.scalar_tensor_tensor(parts[:, t, D:P], msg[:, t, :], c[5], parts[:, t, 0:D], ALU.mult,
                                           ALU.subtract).then_inc(s["parts_made"], 1)

            def epilogue(l, i):
                g = i + l * SB
                for b in range(SBB):
                    dve.wait_ge(s["sums_done"], g * SBB + b + 1)
                    if l and b == 0:
                        dve.wait_ge(s["h_saved"], l * SB)
                    cols = slice(b * NB, (b + 1) * NB)
                    v.scalar_tensor_tensor(zP[:, cols], ps[:, b, 0:NB], scal[:, l, 6:7],
                                           hT[:, ds(i * SBC + b * NB, NB)], ALU.mult, ALU.add).then_inc(s["sums_read"], 1)
                    if l == 0:
                        dve.wait_ge(s["sums_read"], g * SBB + b + 1)
                        v.tensor_scalar(zero_zP[:], zP[:, cols], 0.0, None, ALU.mult).then_inc(s["zeros_made"], 1)
                        dve.wait_ge(s["zeros_made"], g * SBB + b + 1)
                        v.tensor_reduce(finite[:, ds(i * SBB + b, 1)], zero_zP[:], AX.X, ALU.add).then_inc(
                            s["finite_found"], 1)
                for w in range(2):
                    bank = ps[:, 6 + w, 0:7 * D].rearrange("p (k d) -> p k d", d=D)
                    dve.wait_ge(s["m_done"], g * 2 + w + 1)
                    if l < L - 1:
                        t = ds(i * SBT + 7 * w, 7)
                        v.tensor_tensor(msg[:, t, :], bank, b2row[:, l + 1:l + 2, :].to_broadcast([P, 7, D]),
                                        ALU.add).then_inc(s["m_kept"], 1)
                        dve.wait_ge(s["m_kept"], g * 2 + w + 1)
                        v.tensor_reduce(peak[:, ds(i * 2 + w, 1)], msg[:, t, :].rearrange("p k d -> p (k d)"), AX.X,
                                        ALU.max, apply_absolute_value=True).then_inc(s["peak_found"], 1)
                    else:
                        t = slice(7 * w, 7 * w + 7)
                        if w == 0 and not (isinstance(i, int) and i == 0):
                            dve.wait_ge(s["out_stored"], 16 * i)
                        v.tensor_tensor(out_t[:, t, :], bank, bfrow[:].unsqueeze(1).to_broadcast([P, 7, D]),
                                        ALU.add).then_inc(s["m_kept"], 1)
                        dve.wait_ge(s["m_kept"], g * 2 + w + 1)
                        dve.wait_ge(s["x_again"], 16 * i + (32 if isinstance(i, int) and i == SB - 1 else 16))
                        v.tensor_tensor(out_t[:, t, :], out_t[:, t, :], x_t[:, t, :], ALU.add).then_inc(s["out_made"], 1)

            for l in range(L):
                scale_and_split(l, BUILD if l == 0 else 2 * SB)
                epilogue(l, 0)
                with dve.Fori(1, SB - 1) as i:
                    epilogue(l, i)
                epilogue(l, SB - 1)
                if l == 0:
                    dve.wait_ge(s["finite_found"], SB * SBB)
                    link(v.tensor_reduce(good[:, 1:2], finite[:], AX.X, ALU.add), dve)
                    v.tensor_scalar(good[:, 1:2], good[:, 1:2], 0.0, None, ALU.is_equal).then_inc(s["good_made"], 1)
            dve.wait_ge(s["good_shared"], 1)
            link(v.tensor_scalar(good[:, 2:3], good[:, 2:3], float(E), None, ALU.is_equal), dve)
            link(v.tensor_scalar(good[:, 3:4], good[:, 3:4], float(P), None, ALU.is_equal), dve)
            v.tensor_tensor(good_i[:], good[0:1, 2:3], good[0:1, 3:4], ALU.mult).then_inc(s["verdict"], 1)

            def tile(l, i):
                if l == -1 and isinstance(i, int):
                    v.memset(msg[:], 0.0).then_inc(gs["zeros_made"], 1)
                pe_before = tiles_before("tensor", l, i)
                dve.wait_ge(gs["loaded"], tiles_before("loaded", l, i) + TILE_SIGNALS["loaded"][l + 1])
                if l == -1:
                    v.tensor_copy(tile_z, tile_h).then_inc(gs["vector"], 1)
                else:
                    v.tensor_tensor(tile_z, tile_h, tile_agg, ALU.add).then_inc(gs["vector"], 1)
                if 0 <= l < L - 1:
                    dve.wait_ge(gs["tensor"], pe_before + 4)
                    v.tensor_tensor(tile_hn, ps[:, 3, 0:D], b2row[:, l, :], ALU.add).then_inc(gs["vector"], 1)
                dve.wait_ge(gs["tensor"], pe_before + TILE_SIGNALS["tensor"][l + 1])
                if l < L - 1:
                    v.tensor_tensor(tile_m, ps[:, 5, 0:D], b2row[:, l + 1, :], ALU.add).then_inc(gs["vector"], 1)
                else:
                    n = TAIL if isinstance(i, int) else P
                    v.tensor_tensor(tile_m[0:n], ps[0:n, 5, 0:D], bfrow[0:n], ALU.add).then_inc(gs["vector"], 1)
                    dve.wait_ge(gs["vector"], tiles_before("vector", l, i) + 2)
                    v.tensor_tensor(tile_m[0:n], tile_m[0:n], tile_x[0:n], ALU.add).then_inc(gs["vector"], 1)

            def edges(l):
                with dve.Fori(0, EDGE_CHUNKS) as c:
                    dve.wait_ge(es[l]["src_loaded"], c * 16 + 16)
                    v.tensor_copy(e_srcf, e_src).then_inc(es[l]["vector"], 1)
                    dve.wait_ge(es[l]["vector"], c * 7 + 1)
                    v.tensor_scalar(e_diag, ident[:], e_srcf, None, ALU.mult).then_inc(es[l]["vector"], 1)
                    dve.wait_ge(es[l]["tensor"], c * 2 + 1)
                    v.tensor_scalar(e_same, ps[:, 6, 0:P], e_srcf, None, ALU.is_equal).then_inc(es[l]["vector"], 1)
                    dve.wait_ge(es[l]["vector"], c * 7 + 3)
                    dve.wait_ge(gs["below_made"], 1)
                    v.tensor_tensor(e_before, e_same, below, ALU.mult).then_inc(es[l]["vector"], 1)
                    dve.wait_ge(es[l]["vector"], c * 7 + 4)
                    v.tensor_reduce(e_seen, e_before, AX.X, ALU.add).then_inc(es[l]["vector"], 1)
                    dve.wait_ge(es[l]["vector"], c * 7 + 5)
                    v.scalar_tensor_tensor(e_to, e_seen, 65536.0, e_srcf, ALU.mult, ALU.add).then_inc(
                        es[l]["vector"], 1)
                    dve.wait_ge(es[l]["tensor"], c * 2 + 2)
                    dve.wait_ge(es[l]["sums"], c * 16 + 16)
                    v.tensor_tensor(e_agg, e_agg, ps[:, 7, 0:D], ALU.add).then_inc(es[l]["vector"], 1)

            general(dve, tile, edges)

        @block.scalar
        def _(act):
            a = nc.scalar
            act.wait_ge(s["variance_made"], 1)
            a.activation(stat[:, 2, :], stat[:, 1, :], ACT.Sqrt).then_inc(s["root_made"], 1)
            for n in range(-(-KT // 4)):
                w = min(4, KT - 4 * n) * P
                act.wait_ge(s["h0_turned"], n + 1)
                last = a.copy(hT[0:D, n * 4 * P:n * 4 * P + w], ps[0:D, 2 + n % 2, 0:w])
                last.then_inc(s["h0_kept"], 1)

            act.wait_ge(s["weights_loaded"], 16 * 8)

            def keep_tile(i, first):
                for q in range(IPAIRS):
                    u, j, slot = q // PAIRS, q % PAIRS, q % PSLOTS
                    if j == 0 and not first:
                        act.wait_ge(counts_stored[u], i * 16)
                    wait_alone(act, s["pair_multiplied"], i * IPAIRS + q + 1)
                    g = u * TG + 2 * j
                    a.activation(stage[:, g:g + 2, :], ps[:, 2 * slot:2 * slot + 2, 0:LO], ACT.Copy, scale=COUNT_UNIT,
                                 saturate=False).then_inc(s["pair_kept"], 1)
                    if q == 6:
                        act.wait_ge(s["hidden0_done"], i + 1)
                        if not first:
                            act.wait_ge(s["message0_done"], i)
                        a.activation(uS[:], ps[0:D, 6, 0:2 * P], ACT.Relu, bias=b1s[:, 0:1]).then_inc(
                            s["hidden0_kept"], 1)

            keep_tile(0, True)
            with act.Fori(1, BUILD) as i:
                keep_tile(i, False)

            def epilogue(l, i):
                g = i + l * SB
                for b in range(SBB):
                    act.wait_ge(s["u_done"], g * SBB + b + 1)
                    a.activation(U[:, b * NB:(b + 1) * NB], ps[0:D, 4 + b % 2, 0:NB], ACT.Relu,
                                 bias=b1s[:, l:l + 1]).then_inc(s["u_kept"], 1)
                for b in range(SBB):
                    act.wait_ge(s["h_done"], g * SBB + b + 1)
                    if b == 0 and l < L - 1 and not (isinstance(i, int) and g == 0):
                        act.wait_ge(s["h_saved"], g)
                    if b == 0 and l == L - 1:
                        act.wait_ge(s["h_saved"], (L - 1) * SB)
                    a.activation(hN[:, b * NB:(b + 1) * NB], ps[0:D, 4 + b % 2, 0:NB], ACT.Identity,
                                 bias=b2s[:, l:l + 1]).then_inc(s["h_kept"], 1)
                for b in range(SBB if l < L - 1 else 0):
                    act.wait_ge(s["v_done"], g * SBB + b + 1)
                    a.activation(V[:, b * NB:(b + 1) * NB], ps[0:D, 4 + b % 2, 0:NB], ACT.Relu,
                                 bias=b1s[:, l + 1:l + 2]).then_inc(s["v_kept"], 1)

            for l in range(L):
                act.wait_ge(s["scale_made"], l + 1)
                if l == 0:
                    act.wait_ge(s["message_kept"], BUILD)
                for n in range(SPLIT):
                    t = slice(n * SBT, (n + 1) * SBT)
                    a.activation(parts[:, t, 0:D], msg[:, t, :], ACT.Copy, scale=scal[:, l, 5:6]).then_inc(
                        s["upper_made"], 1)
                epilogue(l, 0)
                with act.Fori(1, SB) as i:
                    epilogue(l, i)

            def tile(l, i):
                pe_before = tiles_before("tensor", l, i)
                relu, plain = ACT.Relu, ACT.Identity
                act.wait_ge(gs["tensor"], pe_before + 1)
                a.copy(zT_g, ps[0:D, 0, 0:P]).then_inc(gs["scalar"], 1)
                if l >= 0:
                    act.wait_ge(gs["tensor"], pe_before + 2)
                    a.activation(uT_g, ps[0:D, 1, 0:P], relu, bias=b1s[:, l:l + 1]).then_inc(gs["scalar"], 1)
                    act.wait_ge(gs["tensor"], pe_before + 3)
                    a.activation(hT_g, ps[0:D, 2, 0:P], plain, bias=b2s[:, l:l + 1]).then_inc(gs["scalar"], 1)
                if l < L - 1:
                    act.wait_ge(gs["tensor"], pe_before + (2 if l == -1 else 5))
                    a.activation(vT_g, ps[0:D, 4, 0:P], relu, bias=b1s[:, l + 1:l + 2]).then_inc(gs["scalar"], 1)

            general(act, tile, None)

        @block.tensor
        def _(pe):
            t = nc.tensor
            pe.wait_ge(s["constants_made"], 5)
            pe.wait_ge(s["tops_cast"], 1)
            half = TOP // 2
            for j in range(2):
                last = t.matmul(ps[:, j, 0:half], ones[0:1, :], first_f[:, j * half:(j + 1) * half], start=True, stop=True)
            last.then_inc(s["tops_spread"], 1)
            pe.wait_ge(s["h0_made"], 1)
            for n in range(-(-KT // 4)):
                if n >= 2:
                    pe.wait_ge(s["h0_kept"], n - 1)
                for j in range(min(4, KT - 4 * n)):
                    last = t.transpose(ps[0:D, 2 + n % 2, j * P:(j + 1) * P], msg[:, 4 * n + j, :], ident[:])
                last.then_inc(s["h0_turned"], 1)
            pe.wait_ge(s["keys_made"], 1)
            for n in range(WT):
                if n >= 4:
                    pe.wait_ge(s["keys_kept"], n - 3)
                bank = ps[:, 4 + n % 4, :].bitcast(F16).rearrange("p (a g) -> p a g", a=8)
                for j, key in enumerate((row_key, col_key)):
                    for k in range(2):
                        last = t.transpose(bank[:, 2 * j + k, :], key[:, n, k * P:(k + 1) * P], ident16[:])
                last.then_inc(s["keys_turned"], 1)

            pe.wait_ge(s["weights_loaded"], 16 * 8)
            pe.wait_ge(s["h0_kept"], -(-KT // 4))
            pe.wait_ge(s["keys_kept"], WT)

            def multiply_tile(i, first):
                for q in range(IPAIRS):
                    hot, slot = q % HOTS, q % PSLOTS
                    wait_alone(pe, s["hots_made"], i * IPAIRS + q + 1)
                    if q >= PSLOTS:
                        wait_alone(pe, s["pair_kept"], i * IPAIRS + q - PSLOTS + 1)
                    elif not first:
                        before = max(k for k in range(IPAIRS) if k % PSLOTS == slot)
                        wait_alone(pe, s["pair_kept"], i * IPAIRS + before + 1 - IPAIRS)
                    for k in range(2):
                        prod = ps[:, 2 * slot + k, 0:LO]
                        half = slice(k * OVER, (k + 1) * OVER)
                        t.matmul(prod, hot_r[:, hot, k, :], hot_c[:, hot, k, :], start=True, stop=False)
                        last = t.matmul(prod, hot_r[half, hot, 2, :], hot_c[half, hot, 2, :], start=False, stop=True)
                    last.then_inc(s["pair_multiplied"], 1)
                    if q == 4:
                        wait_alone(pe, s["h_copied"], i + 1)
                        if not first:
                            wait_alone(pe, s["hidden0_kept"], i)
                        t.matmul(ps[0:D, 6, 0:2 * P], W1s[0:D, 0, :], hS[:], start=True, stop=True).then_inc(
                            s["hidden0_done"], 1)
                    if q == 12:
                        wait_alone(pe, s["hidden0_kept"], i + 1)
                        if not first:
                            wait_alone(pe, s["message_kept"], i)
                        for k in range(2):
                            last = t.matmul(ps[:, 7, k * D:(k + 1) * D], uS[:, k * P:(k + 1) * P], W2s[:, 0, :],
                                            start=True, stop=True)
                        last.then_inc(s["message0_done"], 1)

            multiply_tile(0, True)
            with pe.Fori(1, BUILD) as i:
                multiply_tile(i, False)

            def mlp_stage(l, i, n):
                g = i + l * SB
                final = l == L - 1
                steps = ["u01", "u23", "h01", "h23"] + ([] if final else ["v01", "v23"]) + ["m0", "m1"]
                if n >= len(steps):
                    return
                kind, which = steps[n][0], steps[n][1:]
                if kind in "uhv":
                    frm, w, ready, done = {"u": (zP, W1s[:, l, :], "sums_read", "u_done"),
                                           "h": (U, W2s[:, l, :], "u_kept", "h_done"),
                                           "v": (hN, None if final else W1s[0:D, l + 1, :], "h_kept", "v_done")}[kind]
                    for b in (int(c) for c in which):
                        wait_alone(pe, s[ready], g * SBB + b + 1)
                        if kind == "u" and b >= 2:
                            wait_alone(pe, s["u_kept"], g * SBB + b - 1)
                        if kind == "h" and b < 2:
                            wait_alone(pe, s["u_kept"], g * SBB + b + 3)
                        if kind == "h" and b >= 2:
                            wait_alone(pe, s["h_kept"], g * SBB + b - 1)
                        if kind == "v" and b < 2:
                            wait_alone(pe, s["h_kept"], g * SBB + b + 3)
                        if kind == "v" and b >= 2:
                            wait_alone(pe, s["v_kept"], g * SBB + b - 1)
                        t.matmul(ps[0:D, 4 + b % 2, 0:NB], w, frm[:, b * NB:(b + 1) * NB], start=True, stop=True).then_inc(
                            s[done], 1)
                else:
                    w = int(which)
                    if final:
                        frm, weights = hN, Wfs[:]
                        pe.wait_ge(s["h_kept"], (g + 1) * SBB)
                    else:
                        frm, weights = V, W2s[:, l + 1, :]
                        pe.wait_ge(s["v_kept"], (g + 1) * SBB)
                    for k in range(7):
                        c = (7 * w + k) * P
                        last = t.matmul(ps[:, 6 + w, k * D:(k + 1) * D], frm[:, c:c + P], weights, start=True, stop=True)
                    last.then_inc(s["m_done"], 1)

            def multiply_stretch(l, i, first):
                g = i + l * SB
                for c in range(CH):
                    r = c % RING
                    wait_alone(pe, counts_loaded[r], (g * SLOT_LOADS[r] + c // RING + 1) * 16)
                    for k in range(c * CK, (c + 1) * CK):
                        if first and k % SBT == 0:
                            pe.wait_ge(s["parts_made"], l * SPLIT + k // SBT + 1)
                        for b in range(SBB):
                            if k == 0 and not (isinstance(i, int) and g == 0):
                                wait_alone(pe, s["sums_read"], g * SBB + b + 1 - SBB)
                            at = (k % CK) * SBC + b * NB
                            last = t.matmul(ps[:, b, 0:NB], parts[:, k, :], ring[:, r, at:at + NB], start=k == 0,
                                            stop=k == KT - 1)
                            if k == KT - 1:
                                last.then_inc(s["sums_done"], 1)
                    if c < CH - 1:
                        last.then_inc(s["counts_used"], 1)
                    if not first:
                        mlp_stage(l, i - 1, c)

            for l in range(L):
                multiply_stretch(l, 0, True)
                with pe.Fori(1, SB) as i:
                    multiply_stretch(l, i, False)
                for n in range(8):
                    mlp_stage(l, SB - 1, n)

            def tile(l, i):
                act_before = tiles_before("scalar", l, i)
                wait_alone(pe, gs["vector"], tiles_before("vector", l, i) + 1)
                t.transpose(ps[0:D, 0, 0:P], tile_z, ident[:]).then_inc(gs["tensor"], 1)
                wait_alone(pe, gs["scalar"], act_before + 1)
                h = zT_g
                if l >= 0:
                    t.matmul(ps[0:D, 1, 0:P], W1s[0:D, l, :], zT_g, start=True, stop=True).then_inc(gs["tensor"], 1)
                    wait_alone(pe, gs["scalar"], act_before + 2)
                    t.matmul(ps[0:D, 2, 0:P], W2s[:, l, :], uT_g, start=True, stop=True).then_inc(gs["tensor"], 1)
                    if l < L - 1:
                        t.matmul(ps[:, 3, 0:D], uT_g, W2s[:, l, :], start=True, stop=True).then_inc(gs["tensor"], 1)
                    wait_alone(pe, gs["scalar"], act_before + 3)
                    h = hT_g
                if l < L - 1:
                    t.matmul(ps[0:D, 4, 0:P], W1s[0:D, l + 1, :], h, start=True, stop=True).then_inc(gs["tensor"], 1)
                    wait_alone(pe, gs["scalar"], act_before + TILE_SIGNALS["scalar"][l + 1])
                    t.matmul(ps[:, 5, 0:D], vT_g, W2s[:, l + 1, :], start=True, stop=True).then_inc(gs["tensor"], 1)
                else:
                    t.matmul(ps[:, 5, 0:D], h, Wfs[:], start=True, stop=True).then_inc(gs["tensor"], 1)

            def edges(l):
                with pe.Fori(0, EDGE_CHUNKS) as c:
                    wait_alone(pe, es[l]["vector"], c * 7 + 2)
                    t.matmul(ps[:, 6, 0:P], ones[:], e_diag, start=True, stop=True).then_inc(es[l]["tensor"], 1)
                    wait_alone(pe, es[l]["vector"], c * 7 + 3)
                    wait_alone(pe, es[l]["messages"], c * 16 + 16)
                    t.matmul(ps[:, 7, 0:D], e_same, e_msg, start=True, stop=True).then_inc(es[l]["tensor"], 1)

            general(pe, tile, edges)


_INS = ["x", "src", "dst", "L0_gnn_W1", "L0_gnn_b1", "L0_gnn_W2", "L0_gnn_b2", "L0_gnn_Wf", "L0_gnn_bf"]


def kernel(**inputs):
    import numpy as _np
    import concourse.bacc as _bacc
    from concourse import mybir as _mybir
    from concourse.bass_utils import run_bass_kernel_spmd as _run

    nc = _bacc.Bacc("TRN2", target_bir_lowering=False, num_devices=1)
    arrays, args = {}, []
    for name in _INS:
        a = _np.ascontiguousarray(inputs[name])
        arrays[f"in_{name}_dram"] = a
        args.append(nc.dram_tensor(f"in_{name}_dram", a.shape, _mybir.dt.from_np(a.dtype), kind="ExternalInput").ap())
    args.append(nc.dram_tensor("out_dram", (N, D), _mybir.dt.float32, kind="ExternalOutput").ap())
    gnn_kernel(nc, *args)
    r = _run(nc, [arrays], core_ids=[0])
    return r.results[0]["out_dram"]
```

```python
from contextlib import ExitStack

import numpy as np
import concourse.bass as bass
from concourse import mybir
from concourse.alu_op_type import AluOpType as ALU

F32, F16, F8 = mybir.dt.float32, mybir.dt.float16, mybir.dt.float8e4
I32, U16, U8 = mybir.dt.int32, mybir.dt.uint16, mybir.dt.uint8
ACT = mybir.ActivationFunctionType
AX = mybir.AxisListType
ds = bass.ds

P = 128
N, D, L, E = 12500, 64, 3, 400000
KT = -(-N // P)
NP = KT * P
TAIL = N - (KT - 1) * P

GN = 4
HALF = NP // 2
HALF_T = KT // 2
HI = P // GN
LO = HALF // HI
TG = P // GN
MAIN, OVER = 128, 64
WIN = MAIN + OVER
GRAN = 16
ROWS = E // GRAN
FAN = 32
TOP = -(-ROWS // FAN)
LAST_START = ROWS - WIN // GRAN
WT = -(-KT * TG // P)
PAIRS = TG // 2
TRIO = 3
BATCH = 2
MAINS = 2 * BATCH
BKEYS = BATCH * TRIO
KINDS = 3
KEYS = KINDS * PAIRS * TRIO
NIBBLE = 16
COUNT_UNIT = 2.0 ** -9
LO_BITS = 9
PK = 100
PC = E // PK
ROUND = 12582912.0
BIG = 1 << 24

HOTS = 4
PSLOTS = 3
BUILD = KT // 2
TB = PAIRS // BATCH
IB = 2 * TB
KEEP_LAG = 2
WITH = LO + 2

NB = 448
SBB = 4
SBC = NB * SBB
SBH = SBC // 2
SBT = SBC // P
SB = NP // SBC
CK = 7
CH = KT // CK
RING = 4
WIDE = 2
SLOT_LOADS = [len(range(s, CH, RING)) for s in range(RING)]
SPLIT = SB
EPS = 1e-5
LN_SUM_TO_MEAN = 1.0 / D


def gnn_kernel(nc, x, src, dst, W1, b1, W2, b2, Wf, bf, out):
    ctx = ExitStack()
    with ctx:
        def sb(name, shape, dt):
            return ctx.enter_context(nc.sbuf_tensor(name, shape, dt))

        def sem(name):
            return ctx.enter_context(nc.semaphore(name))

        def scratch(name, shape, dt):
            return nc.dram_tensor(name, shape, dt, kind="Internal").ap()

        counts_dram = scratch("counts_dram", (KT, TG, P, LO), U8)
        firsts_dram = scratch("firsts_dram", (TOP * FAN,), I32)
        packed_dram = scratch("packed_dram", (E,), I32)
        h0_dram = scratch("h0_dram", (NP, D), F32)
        h_dram = scratch("h_dram", (NP, D), F32)
        m_dram = scratch("m_dram", (NP, D), F32)
        agg_dram = scratch("agg_dram", (NP, D), F32)
        counts_rows = counts_dram.rearrange("k g p n -> (k g p n)").rearrange(
            "(c k r s) -> c r k s", k=CK, r=P, s=HALF)

        hT = sb("hT", [P, NP], F32)
        msg = sb("msg", [P, KT, D], F32)
        parts = sb("parts", [P, KT, P], F16)
        W1s = sb("W1s", [P, L, D], F32)
        W2s = sb("W2s", [D, L, D], F32)
        Wfs = sb("Wfs", [D, D], F32)
        b1s = sb("b1s", [D, L], F32)
        b2s = sb("b2s", [D, L], F32)
        b2row = sb("b2row", [P, L, D], F32)
        bfrow = sb("bfrow", [P, D], F32)
        ident = sb("ident", [P, P], F32)
        ident16 = sb("ident16", [P, P], F16)
        ones = sb("ones", [P, P], F32)
        ones16 = sb("ones16", [P, 2], F16)
        iota = sb("iota", [P, LO], F16)
        node_i = sb("node_i", [P, WT], I32)
        node = sb("node", [P, WT], F32)
        node_hi = sb("node_hi", [P, WT], F32)
        cnt = sb("cnt", [P, WT], F32)
        row = sb("row", [P, WT], F32)
        row_i = sb("row_i", [P, WT], I32)
        start_i = sb("start_i", [P, WT], I32)
        stat = sb("stat", [P, 4, KT], F32)
        peak = sb("peak", [P, BUILD], F32)
        scal = sb("scal", [P, L, 8], F32)
        good = sb("good", [P, 4], F32)
        good_i = sb("good_i", [1, 1], I32)
        pad_i = sb("pad_i", [1, TOP * FAN - ROWS], I32)

        ARENA = 95232
        arena = sb("arena", [P, ARENA], U8)

        def view(at, shape, dt, rows=P):
            size = {F32: 4, I32: 4, F16: 2, U8: 1}[dt]
            n = size * int(np.prod(shape))
            assert at % 4 == 0 and at + n <= ARENA
            v = arena[0:rows, at:at + n].bitcast(dt)
            if len(shape) == 2:
                v = v.rearrange("p (a b) -> p a b", a=shape[0])
            if len(shape) == 3:
                v = v.rearrange("p (a b c) -> p a b c", a=shape[0], b=shape[1])
            return v, at + n

        dst_t, at = view(0, [PC], I32, PK)
        src_t, at = view(at, [PC], I32, PK)
        pa, at = view(at, [PC], F32, PK)
        pb, at = view(at, [PC], F32, PK)
        pc, at = view(at, [PC], I32, PK)
        firsts, at = view(at, [ROWS // PK], I32, PK)
        first_i, at = view(at, [TOP], I32, 1)
        first_f, at = view(at, [TOP], F32, 1)
        keys, at = view(0, [4 * WT, KEYS], F16)
        win, end = view(at, [WT, WIN], I32)
        win_row, end = view(end, [WT, WIN], I32)
        win_rowf = win_row.bitcast(F32)
        fan, end = view(end, [WT, FAN], I32)
        fan_f, _ = view(at, [WT, FAN], F32)
        compare, _ = view(at, [TOP], F32)
        col_key, end = view(ARENA - 2 * KINDS * WT * 2 * P, [WT, 2 * P], F16)
        row_key, end = view(end, [WT, 2 * P], F16)
        weight, end = view(end, [WT, 2 * P], F16)
        assert end <= ARENA
        hot_c, at = view(at, [HOTS, BKEYS, WITH], F16)
        hot_r, at = view(at, [HOTS, BKEYS, P], F16)
        stage, at = view(at, [2 * TG, LO], U8)
        key_now = sb("key_now", [P, 2, KEYS, 2], F16)
        over_weight = sb("over_weight", [P, 2, TB, BATCH], F32)
        hS = sb("hS", [D, 2 * P], F32)
        uS = sb("uS", [D, 2 * P], F32)
        row_edges, _ = view(ARENA - 2 * BUILD * IB * 2 * BATCH, [BUILD * IB, 2 * BATCH], F16)
        ring, at = view(0, [RING, CK * SBH], U8)
        spread, at = view(at, [WIDE, 2, CK * SBH], U8)
        zP, at = view(at, [SBC], F32)
        U, at = view(at, [SBC], F32, D)
        hN, at = view(at, [SBC], F32, D)
        V, at = view(at, [SBC], F32, D)
        x_t, at = view(at, [SBT, D], F32)
        out_t, at = view(at, [SBT, D], F32)
        tile_h, at = view(0, [D], F32)
        tile_agg, at = view(at, [D], F32)
        tile_x, at = view(at, [D], F32)
        tile_z, at = view(at, [D], F32)
        tile_hn, at = view(at, [D], F32)
        tile_m, at = view(at, [D], F32)
        zT_g, at = view(at, [P], F32, D)
        uT_g, at = view(at, [P], F32, D)
        hT_g, at = view(at, [P], F32, D)
        vT_g, at = view(at, [P], F32, D)
        e_dst, at = view(at, [1], I32)
        e_src, at = view(at, [1], I32)
        e_to, at = view(at, [1], I32)
        e_srcf, at = view(at, [1], F32)
        e_seen, at = view(at, [1], F32)
        e_msg, at = view(at, [D], F32)
        e_agg, at = view(at, [D], F32)
        e_diag, at = view(at, [P], F32)
        e_same, at = view(at, [P], F32)
        e_before, at = view(at, [P], F32)
        below, at = view(at, [P], F32)

        ps = ctx.enter_context(nc.psum_tensor("ps", [P, 8, 512], F32))

        s = {n: sem(n) for n in (
            "dst_loaded", "src_loaded", "x_loaded", "weights_loaded", "constants_made", "pad_made", "x_padded",
            "firsts_made", "firsts_stored", "tops_loaded", "tops_cast", "tops_spread",
            "packed_made", "packed_stored", "rows_found", "fans_gathered", "starts_found", "windows_gathered",
            "vector_chain", "variance_made", "root_made", "h0_made", "h0_stored", "h0_turned", "h0_kept", "h_zeroed",
            "keys_made", "keys_turned", "keys_kept", "keys_copied", "overs_copied", "rows_made", "hots_made", "overs_weighted", "inverses_made", "batch_multiplied", "batch_kept",
            "counts_stored_0", "counts_stored_1",
            "h_copied", "hidden0_done", "hidden0_kept", "message0_done", "message_kept",
            "peak_found", "peak_made", "peak_shared", "scale_made", "upper_made", "parts_made",
            "counts_unpacked", "counts_used", "sums_done", "sums_read", "u_done", "u_kept", "h_done", "h_kept", "h_saved",
            "v_done", "v_kept", "m_done", "m_kept", "x_again", "out_done", "out_made", "out_read", "out_stored",
            "good_made", "good_shared", "verdict",
        )}
        gs = {n: sem("general_" + n) for n in (
            "tensor", "scalar", "vector", "loaded", "stored", "zeros_made", "agg_cleared", "below_made")}
        es = [{n: sem(f"edges_{n}_{l}") for n in (
            "dst_loaded", "src_loaded", "messages", "sums", "vector", "tensor", "added")} for l in range(L)]
        counts_loaded = [sem(f"counts_loaded_{r}") for r in range(RING)]
        counts_stored = [s["counts_stored_0"], s["counts_stored_1"]]

        chain = [0]

        def link(ins, eng):
            chain[0] += 1
            ins.then_inc(s["vector_chain"], 1)
            eng.wait_ge(s["vector_chain"], chain[0])

        passed = {e: sem(f"waits_passed_{e}") for e in ("sync", "scalar", "tensor", "gpsimd")}


        def wait_alone(eng, semaphore, value):
            eng.wait_ge(semaphore, value)
            if not isinstance(value, int):
                eng.sem_inc(passed[{"SP": "sync", "Activation": "scalar", "PE": "tensor", "Pool": "gpsimd"}[eng.engine.name]], 1)

        TILE_SIGNALS = {"tensor": [3] + [6] * (L - 1) + [4], "scalar": [2] + [4] * (L - 1) + [3],
                        "vector": [2] + [3] * (L - 1) + [3], "loaded": [16] + [32] * (L - 1) + [48],
                        "stored": [16] + [32] * (L - 1) + [16]}
        EDGE_CHUNKS = E // P

        def tiles_before(kind, l, t):
            each = TILE_SIGNALS[kind]
            return t * each[l + 1] + KT * sum(each[:l + 1])

        def general(eng, tile, edges):
            eng.wait_ge(s["verdict"], 1)
            fine = eng.value_load(good_i[0:1, 0:1], min_val=0, max_val=1)
            with eng.If(fine < 1):
                for l in range(-1, L):
                    if tile is not None:
                        with eng.Fori(0, KT - 1) as i:
                            tile(l, i)
                        tile(l, KT - 1)
                    if edges is not None and l < L - 1:
                        edges(l + 1)

        block = ctx.enter_context(nc.Block())

        @block.sync
        def _(sp):
            sp.dma_start(dst_t, dst.rearrange("(p c) -> p c", p=PK)).then_inc(s["dst_loaded"], 16)
            sp.dma_start(src_t, src.rearrange("(p c) -> p c", p=PK)).then_inc(s["src_loaded"], 16)
            weights = [(W1s[0:D], W1.rearrange("l k m -> k l m")), (W1s[D:P], W1.rearrange("l k m -> k l m")),
                       (W2s[:], W2.rearrange("l k m -> k l m")), (Wfs[:], Wf), (b1s[:], b1.rearrange("l d -> d l")),
                       (b2s[:], b2.rearrange("l d -> d l")),
                       (b2row[:], b2.rearrange("l d -> (l d)").partition_broadcast(P)), (bfrow[:], bf.partition_broadcast(P))]
            for to, frm in weights:
                if to.ndim == 3 and to.shape[0] == P and frm.ndim == 2:
                    to = to.rearrange("p l d -> p (l d)")
                with nc.allow_non_contiguous_dma(reason="192 biases"):
                    sp.dma_start(to, frm).then_inc(s["weights_loaded"], 16)
            sp.wait_ge(s["firsts_made"], 1)
            sp.wait_ge(s["pad_made"], 1)
            sp.dma_start(firsts_dram[0:ROWS].rearrange("(p c) -> p c", p=PK), firsts).then_inc(s["firsts_stored"], 16)
            sp.dma_start(firsts_dram[ROWS:].rearrange("(p c) -> p c", p=1), pad_i[:]).then_inc(s["firsts_stored"], 16)
            sp.wait_ge(s["firsts_stored"], 32)
            with nc.allow_non_contiguous_dma(reason="one number of each row"):
                sp.dma_start(first_i, firsts_dram.rearrange("(p r f) -> p r f", p=1, f=FAN)[:, :, 0]).then_inc(
                    s["tops_loaded"], 16)
            sp.wait_ge(s["packed_made"], 1)
            sp.dma_start(packed_dram.rearrange("(p c) -> p c", p=PK), pc).then_inc(s["packed_stored"], 16)
            sp.wait_ge(s["h0_made"], 1)
            sp.dma_start(h0_dram.rearrange("(k p) d -> p k d", p=P), msg[:]).then_inc(s["h0_stored"], 16)

            with sp.Fori(0, BUILD) as i:
                for u in range(2):
                    wait_alone(sp, s["batch_kept"], i * IB + (u + 1) * TB)
                    sp.dma_start(counts_dram[ds(i * 2 + u, 1)].rearrange("k g p n -> p (k g) n"),
                                 stage[:, u * TG:(u + 1) * TG, :]).then_inc(counts_stored[u], 16)

            sp.wait_ge(counts_stored[0], 16 * BUILD)
            sp.wait_ge(counts_stored[1], 16 * BUILD)

            def load_stretch(sbase, l, first):
                g = sbase + l * SB
                for c in range(CH):
                    r = c % RING
                    if c >= RING:
                        wait_alone(sp, s["counts_unpacked"], g * CH + (c - RING + 1))
                    elif not first:
                        before = max(k for k in range(CH) if k % RING == r)
                        wait_alone(sp, s["counts_unpacked"], g * CH + (before + 1 - CH))
                    sp.dma_start(ring[:, r, :].rearrange("p (k n) -> p k n", k=CK),
                                 counts_rows[c][:, :, ds(sbase * SBH, SBH)]).then_inc(counts_loaded[r], 16)

            def load_x(sbase):
                for w in range(2):
                    sp.dma_start(x_t[:, 7 * w:7 * w + 7, :],
                                 x[ds((sbase - 1) * SBH + w * HALF, SBH), :].rearrange("(k p) d -> p k d", p=P)).then_inc(
                        s["x_again"], 16)

            for l in range(L):
                load_stretch(0, l, l == 0)
                with sp.Fori(1, SB) as i:
                    if l == L - 1:
                        load_x(i)
                    load_stretch(i, l, False)
                    if l == L - 1:
                        wait_alone(sp, s["out_made"], 2 * i)
                        for w in range(2):
                            sp.dma_start(out[ds((i - 1) * SBH + w * HALF, SBH), :].rearrange("(k p) d -> p k d", p=P),
                                         out_t[:, 7 * w:7 * w + 7, :]).then_inc(s["out_stored"], 16)
            sp.wait_ge(s["out_made"], 2 * (SB - 1))
            last = (SB - 1) * SBH
            pieces = [(slice(0, 7), last, P), (slice(7, SBT - 1), last + HALF, P), (slice(SBT - 1, SBT), (KT - 1) * P, TAIL)]
            for t, at, n in pieces:
                rows = (t.stop - t.start - 1) * P + n
                sp.dma_start(x_t[0:n, t, :], x[at:at + rows, :].rearrange("(k p) d -> p k d", p=n)).then_inc(
                    s["x_again"], 16)
            sp.wait_ge(s["out_made"], 2 * SB)
            for t, at, n in pieces:
                rows = (t.stop - t.start - 1) * P + n
                sp.dma_start(out[at:at + rows, :].rearrange("(k p) d -> p k d", p=n), out_t[0:n, t, :]).then_inc(
                    s["out_stored"], 16)
            sp.wait_ge(s["out_stored"], 16 * (2 * (SB - 1) + 3))
            sp.wait_ge(s["h0_stored"], 16)

            def tile(l, i):
                rows = ds(i * P, P)
                n = TAIL if isinstance(i, int) else P
                sp.dma_start(tile_h, (h0_dram if l <= 0 else h_dram)[rows, :]).then_inc(gs["loaded"], 16)
                if l >= 0:
                    sp.dma_start(tile_agg, agg_dram[rows, :]).then_inc(gs["loaded"], 16)
                if l == L - 1:
                    sp.dma_start(tile_x[0:n], x[ds(i * P, n), :]).then_inc(gs["loaded"], 16)
                before = tiles_before("vector", l, i)
                if 0 <= l < L - 1:
                    wait_alone(sp, gs["vector"], before + 2)
                    sp.dma_start(h_dram[rows, :], tile_hn).then_inc(gs["stored"], 16)
                wait_alone(sp, gs["vector"], before + TILE_SIGNALS["vector"][l + 1])
                if l < L - 1:
                    sp.dma_start(m_dram[rows, :], tile_m).then_inc(gs["stored"], 16)
                else:
                    sp.dma_start(out[ds(i * P, n), :], tile_m[0:n]).then_inc(gs["stored"], 16)
                wait_alone(sp, gs["stored"], tiles_before("stored", l, i) + TILE_SIGNALS["stored"][l + 1])

            def edges(l):
                sp.wait_ge(gs["stored"], tiles_before("stored", l, 0))
                sp.wait_ge(gs["zeros_made"], 1)
                sp.dma_start(agg_dram.rearrange("(k p) d -> p k d", p=P), msg[:]).then_inc(gs["agg_cleared"], 16)
                sp.wait_ge(gs["agg_cleared"], 16 * (l + 1))
                with sp.Fori(0, EDGE_CHUNKS) as c:
                    sp.dma_start(e_dst, dst[ds(c * P, P)].unsqueeze(1)).then_inc(es[l]["dst_loaded"], 16)
                    sp.dma_start(e_src, src[ds(c * P, P)].unsqueeze(1)).then_inc(es[l]["src_loaded"], 16)
                    wait_alone(sp, es[l]["added"], c * 16 + 16)

            general(sp, tile, edges)

        @block.gpsimd
        def _(pool):
            nc.gpsimd.memset(msg[:, KT - 1, :], 0.0).then_inc(s["x_padded"], 1)
            pool.wait_ge(s["x_padded"], 1)
            pool.dma_start(msg[:, 0:KT - 1, :], x[0:(KT - 1) * P, :].rearrange("(k p) d -> p k d", p=P)).then_inc(
                s["x_loaded"], 16)
            pool.dma_start(msg[0:TAIL, KT - 1, :], x[(KT - 1) * P:N, :]).then_inc(s["x_loaded"], 16)
            nc.gpsimd.memset(pad_i[:], BIG).then_inc(s["pad_made"], 1)
            nc.gpsimd.memset(ones16[:], 1.0).then_inc(s["constants_made"], 1)
            nc.gpsimd.memset(ones[:], 1.0).then_inc(s["constants_made"], 1)
            nc.gpsimd.iota(iota[:], pattern=[[1, LO]], base=0, channel_multiplier=0,
                           allow_small_or_imprecise_dtypes=True).then_inc(s["constants_made"], 1)
            nc.gpsimd.iota(node_i[:], pattern=[[GN * P, WT]], base=0, channel_multiplier=GN).then_inc(
                s["constants_made"], 1)
            pool.wait_ge(s["constants_made"], 4)
            nc.gpsimd.affine_select(out=ident[:], in_=ones[:], compare_op=ALU.is_equal, fill=0.0, base=0,
                                    pattern=[[-1, P]], channel_multiplier=1).then_inc(s["constants_made"], 1)
            pool.wait_ge(s["constants_made"], 5)
            nc.gpsimd.tensor_copy(ident16[:], ident[:]).then_inc(s["constants_made"], 1)
            pool.wait_ge(s["constants_made"], 6)
            nc.gpsimd.memset(hT[D:P, :], 0.0).then_inc(s["h_zeroed"], 1)
            pool.wait_ge(s["h_zeroed"], 1)

            pool.wait_ge(s["rows_found"], 1)
            pool.wait_ge(s["firsts_stored"], 32)
            for t in range(WT):
                pool.indirect_dma_start(fan[:, t, :], None, firsts_dram.rearrange("(r f) -> r f", f=FAN),
                                        bass.IndirectOffsetOnAxis(ap=row_i[:, t:t + 1], axis=0)).then_inc(
                    s["fans_gathered"], 16)
            pool.wait_ge(s["starts_found"], 1)
            pool.wait_ge(s["packed_stored"], 16)
            for t in range(WT):
                pool.indirect_dma_start(win[:, t, :], None, packed_dram.rearrange("(r f) -> r f", f=GRAN),
                                        bass.IndirectOffsetOnAxis(ap=start_i[:, t:t + 1], axis=0)).then_inc(
                    s["windows_gathered"], 16)

            pool.wait_ge(s["h0_kept"], -(-KT // 4))
            pool.wait_ge(s["keys_kept"], WT)

            def copy_keys(i, u, first):
                if not first:
                    pool.wait_ge(s["hots_made"], ((i - 1) * 2 + u + 1) * TB)
                tile_keys = keys[:, ds(i * 2 + u, 1), :].rearrange("p a k -> p (a k)")
                nc.gpsimd.tensor_copy(key_now[:, u, :, :], tile_keys.unsqueeze(2).to_broadcast([P, KEYS, 2])).then_inc(
                    s["keys_copied"], 1)
                if not first:
                    pool.wait_ge(s["overs_weighted"], ((i - 1) * 2 + u + 1) * TB)
                weights = tile_keys[:, 2 * PAIRS * TRIO:].rearrange("p (b c) -> p b c", c=BKEYS)[:, :, MAINS:BKEYS]
                nc.gpsimd.tensor_copy(over_weight[:, u, :, :], weights).then_inc(s["overs_copied"], 1)

            def prepare(i, first):
                if not first:
                    pool.wait_ge(s["hidden0_done"], i)
                nc.gpsimd.tensor_copy(hS[:], hT[0:D, ds(i * 2 * P, 2 * P)]).then_inc(s["h_copied"], 1)
                for q in range(IB):
                    u, slot = q // TB, q % HOTS
                    if q == 0 or q == TB:
                        wait_alone(pool, s["keys_copied"], i * 2 + u + 1)
                    if not first or q >= HOTS:
                        wait_alone(pool, s["batch_multiplied"], i * IB + q - HOTS + 1)
                    k = (2 * TB + q % TB) * BKEYS
                    nc.gpsimd.tensor_scalar(hot_c[:, slot, :, LO], key_now[:, u, k:k + BKEYS, 0], -1.0 / NIBBLE,
                                            1.0 + 1.0 / NIBBLE, ALU.mult, ALU.add).then_inc(s["inverses_made"], 1)
                    if q % TB == TB - 1:
                        pool.wait_ge(s["inverses_made"], i * IB + q + 1)
                        copy_keys(i + 1, u, False)

            copy_keys(0, 0, True)
            copy_keys(0, 1, True)
            prepare(0, True)
            with pool.Fori(1, BUILD) as i:
                prepare(i, False)

            for l in range(L):
                pool.wait_ge(s["peak_made"], l + 1)
                nc.gpsimd.partition_all_reduce(scal[:, l, 1:2], scal[:, l, 0:1], P, bass.bass_isa.ReduceOp.max).then_inc(
                    s["peak_shared"], 1)
                if l == L - 1:
                    break
                with pool.Fori(0, SB) as i:
                    pool.wait_ge(s["h_kept"], (i + l * SB) * SBB + SBB)
                    for w in range(2):
                        nc.gpsimd.tensor_copy(hT[0:D, ds(i * SBH + w * HALF, SBH)], hN[:, w * SBH:(w + 1) * SBH]).then_inc(
                            s["h_saved"], 1)
            pool.wait_ge(s["good_made"], 1)
            nc.gpsimd.partition_all_reduce(good[:, 2:4], good[:, 0:2], P, bass.bass_isa.ReduceOp.add).then_inc(
                s["good_shared"], 1)

            def edges(l):
                if l == 0:
                    nc.gpsimd.affine_select(out=below, in_=ones[:], compare_op=ALU.is_gt, fill=0.0, base=0,
                                            pattern=[[-1, P]], channel_multiplier=1).then_inc(gs["below_made"], 1)
                with pool.Fori(0, EDGE_CHUNKS) as c:
                    wait_alone(pool, es[l]["dst_loaded"], c * 16 + 16)
                    pool.indirect_dma_start(e_msg, None, m_dram, bass.IndirectOffsetOnAxis(ap=e_dst, axis=0)).then_inc(
                        es[l]["messages"], 16)
                    wait_alone(pool, es[l]["src_loaded"], c * 16 + 16)
                    pool.indirect_dma_start(e_agg, None, agg_dram, bass.IndirectOffsetOnAxis(ap=e_src, axis=0)).then_inc(
                        es[l]["sums"], 16)
                    wait_alone(pool, es[l]["vector"], c * 7 + 7)
                    pool.indirect_dma_start(agg_dram, bass.IndirectOffsetOnAxis(ap=e_to, axis=0), e_agg, None,
                                            bounds_check=NP - 1, oob_is_err=False).then_inc(es[l]["added"], 16)

            general(pool, None, edges)

        @block.vector
        def _(dve):
            v = nc.vector
            dve.wait_ge(s["dst_loaded"], 16)
            v.tensor_copy(firsts, dst_t.rearrange("p (c g) -> p c g", g=GRAN)[:, :, 0]).then_inc(s["firsts_made"], 1)
            dve.wait_ge(s["src_loaded"], 16)
            link(v.tensor_scalar(pa, src_t, 1.0 / LO, -0.5 + 1.0 / 1024, ALU.mult, ALU.add), dve)
            link(v.tensor_scalar(pb, pa, ROUND, ROUND, ALU.add, ALU.subtract), dve)
            link(v.scalar_tensor_tensor(pc, pb, -float(LO), src_t, ALU.mult, ALU.add), dve)
            link(v.tensor_scalar(pa, src_t, float(HALF), HI - 0.5, ALU.is_ge, ALU.mult), dve)
            link(v.tensor_tensor(pb, pb, pa, ALU.subtract), dve)
            link(v.scalar_tensor_tensor(pa, dst_t, float(HI), pb, ALU.mult, ALU.add), dve)
            link(v.tensor_scalar(dst_t, pa, float(1 << LO_BITS), None, ALU.mult), dve)
            v.tensor_tensor(pc, dst_t, pc, ALU.bitwise_or).then_inc(s["packed_made"], 1)

            dve.wait_ge(s["constants_made"], 4)
            link(v.tensor_copy(node[:], node_i[:]), dve)
            link(v.tensor_scalar(node_hi[:], node[:], float(HI), None, ALU.mult), dve)
            dve.wait_ge(s["tops_loaded"], 16)
            v.tensor_copy(first_f, first_i).then_inc(s["tops_cast"], 1)
            dve.wait_ge(s["tops_spread"], 1)
            dve.wait_ge(s["packed_stored"], 16)
            half = TOP // 2
            tops = ps[:, 0:2, 0:half]
            comp = compare.rearrange("p (a b) -> p a b", a=2)
            for t in range(WT):
                link(v.tensor_scalar(comp, tops, node[:, t:t + 1], None, ALU.is_lt), dve)
                link(v.tensor_reduce(cnt[:, t:t + 1], comp, AX.XY, ALU.add), dve)
            link(v.tensor_scalar(row[:], cnt[:], -1.0, 0.0, ALU.add, ALU.max), dve)
            v.tensor_copy(row_i[:], row[:]).then_inc(s["rows_found"], 1)

            dve.wait_ge(s["x_loaded"], 32)
            sq = parts[:].rearrange("p k c -> p (k c)").bitcast(F32).rearrange("p (k d) -> p k d", d=D)
            mean, var, inv, tmp = (stat[:, j, :] for j in range(4))

            def wide(a):
                return a.unsqueeze(2).to_broadcast([P, KT, D])

            link(v.tensor_reduce(mean, msg[:], AX.X, ALU.add), dve)
            link(v.tensor_scalar(mean, mean, LN_SUM_TO_MEAN, None, ALU.mult), dve)
            link(v.tensor_tensor(msg[:], msg[:], wide(mean), ALU.subtract), dve)
            link(v.tensor_tensor(sq, msg[:], msg[:], ALU.mult), dve)
            link(v.tensor_reduce(var, sq, AX.X, ALU.add), dve)
            v.tensor_scalar(var, var, LN_SUM_TO_MEAN, EPS, ALU.mult, ALU.add).then_inc(s["variance_made"], 1)
            dve.wait_ge(s["root_made"], 1)
            link(v.reciprocal(inv, inv), dve)
            link(v.tensor_tensor(tmp, inv, inv, ALU.mult), dve)
            link(v.tensor_tensor(tmp, tmp, var, ALU.mult), dve)
            link(v.tensor_scalar(tmp, tmp, -0.5, 1.5, ALU.mult, ALU.add), dve)
            link(v.tensor_tensor(inv, inv, tmp, ALU.mult), dve)
            v.scalar_tensor_tensor(msg[:], msg[:], 0.0, wide(inv), ALU.max, ALU.mult).then_inc(s["h0_made"], 1)

            dve.wait_ge(s["fans_gathered"], 16 * WT)
            nodes = node[:].unsqueeze(2).to_broadcast([P, WT, FAN])
            link(v.tensor_tensor(fan_f, fan, nodes, ALU.is_lt), dve)
            link(v.tensor_reduce(cnt[:], fan_f, AX.X, ALU.add), dve)
            link(v.tensor_scalar(cnt[:], cnt[:], -1.0, 0.0, ALU.add, ALU.max), dve)
            link(v.scalar_tensor_tensor(row[:], row[:], float(FAN), cnt[:], ALU.mult, ALU.add), dve)
            v.tensor_scalar(start_i[:], row[:], float(LAST_START), None, ALU.min).then_inc(s["starts_found"], 1)

            dve.wait_ge(s["windows_gathered"], 16 * WT)
            link(v.tensor_scalar(win_row, win, LO_BITS, None, ALU.arith_shift_right), dve)
            link(v.tensor_scalar(win, win, (1 << LO_BITS) - 1, None, ALU.bitwise_and), dve)
            link(v.tensor_tensor(win_rowf, win_row, node_hi[:].unsqueeze(2).to_broadcast([P, WT, WIN]),
                                 ALU.subtract), dve)
            link(v.tensor_scalar(row_key[:, :, 0:WIN], win_rowf, float(P), -1.0, ALU.min, ALU.max), dve)
            link(v.tensor_scalar(win_rowf, win, float(1 << (LO_BITS - 1)), NIBBLE - 1.0, ALU.is_ge, ALU.mult), dve)
            link(v.tensor_scalar(weight[:, :, 0:WIN], win_rowf, 1.0, None, ALU.add), dve)
            link(v.tensor_scalar(win, win, (1 << (LO_BITS - 1)) - 1, None, ALU.bitwise_and), dve)
            link(v.tensor_copy(col_key[:, :, 0:WIN], win), dve)
            for key in (row_key, weight):
                link(v.tensor_copy(key[:, :, WIN:2 * P], key[:, :, MAIN:WIN]), dve)
            v.tensor_copy(col_key[:, :, WIN:2 * P], col_key[:, :, MAIN:WIN]).then_inc(s["keys_made"], 1)

            for t in range(WT):
                dve.wait_ge(s["keys_turned"], t + 1)
                bank = ps[:, 4 + t % 4, :].bitcast(F16).rearrange("p (a g) -> p a g", a=8)
                to = keys[:, 4 * t:4 * t + 4, :]
                for j in range(KINDS):
                    kind = to[:, :, j * PAIRS * TRIO:(j + 1) * PAIRS * TRIO].rearrange("p k (b c) -> p k b c", c=BKEYS)
                    v.tensor_copy(kind[:, :, :, 0:MAINS],
                                  bank[:, 2 * j, :].rearrange("p (k b c) -> p k b c", k=4, c=MAINS))
                    over = bank[:, 2 * j + 1, :].rearrange("p (k b pair two) -> p k b pair two", k=4, pair=BATCH, two=2)
                    v.tensor_copy(kind[0:OVER, :, :, MAINS:BKEYS], over[0:OVER, :, :, :, 0])
                    last = v.tensor_copy(kind[OVER:P, :, :, MAINS:BKEYS], over[OVER:P, :, :, :, 1])
                last.then_inc(s["keys_kept"], 1)
            dve.wait_ge(s["keys_kept"], WT)

            def hot_tile(i, first):
                def compare_keys(out, width, key):
                    v_shape = [P, BKEYS, width // 2, 2]
                    return v.tensor_tensor(
                        out.rearrange("p c (m two) -> p c m two", two=2),
                        iota[:, 0:width].rearrange("p (m two) -> p m two", two=2).unsqueeze(1).to_broadcast(v_shape),
                        key.unsqueeze(2).to_broadcast(v_shape), ALU.is_equal)

                v_shape = [P, MAINS, P // 2, 2]
                for q in range(IB):
                    u, slot = q // TB, q % HOTS
                    if q % TB == 0:
                        dve.wait_ge(s["keys_copied"], i * 2 + u + 1)
                    if not first or q >= HOTS:
                        dve.wait_ge(s["batch_multiplied"], i * IB + q - HOTS + 1)
                    k = [(n * TB + q % TB) * BKEYS for n in range(KINDS)]
                    compare_keys(hot_r[:, slot, :, :], P, key_now[:, u, k[0]:k[0] + BKEYS, :]).then_inc(s["rows_made"], 1)
                    compare_keys(hot_c[:, slot, :, 0:LO], LO, key_now[:, u, k[1]:k[1] + BKEYS, :])
                    dve.wait_ge(s["rows_made"], i * IB + q + 1)
                    rows = hot_r[:, slot, 0:MAINS, :].rearrange("p c (m two) -> p c m two", two=2)
                    v.tensor_tensor(rows, rows, key_now[:, u, k[2]:k[2] + MAINS, :].unsqueeze(2).to_broadcast(v_shape),
                                    ALU.mult).then_inc(s["hots_made"], 1)
                    if q == 8:
                        dve.wait_ge(s["message0_done"], i + 1)
                        v.tensor_tensor(msg[:, ds(i * 2, 2), :], ps[:, 7, 0:2 * D].rearrange("p (k d) -> p k d", k=2),
                                        b2row[:, 0:1, :].to_broadcast([P, 2, D]), ALU.add).then_inc(s["message_kept"], 1)
                    if q == 9:
                        dve.wait_ge(s["message_kept"], i + 1)
                        v.tensor_reduce(peak[:, ds(i, 1)], msg[:, ds(i * 2, 2), :].rearrange("p k d -> p (k d)"), AX.X,
                                        ALU.max, apply_absolute_value=True).then_inc(s["peak_found"], 1)

            dve.wait_ge(s["h0_stored"], 16)
            hot_tile(0, True)
            with dve.Fori(1, BUILD) as i:
                hot_tile(i, False)

            def judge():
                v.tensor_reduce(good[:, 0:1], row_edges, AX.XY, ALU.add)
                link(v.tensor_reduce(good[:, 1:2], row_edges, AX.XY, ALU.max), dve)
                v.tensor_scalar(good[:, 1:2], good[:, 1:2], NIBBLE - 1.0, None, ALU.is_le).then_inc(s["good_made"], 1)

            def scale_and_split(l, peaks):
                c = [scal[:, l, j:j + 1] for j in range(8)]
                dve.wait_ge(s["peak_found"], BUILD + l * 2 * SB)
                v.tensor_reduce(c[0], peak[:, 0:peaks], AX.X, ALU.max).then_inc(s["peak_made"], 1)
                dve.wait_ge(s["peak_shared"], l + 1)
                link(v.tensor_scalar(c[2], c[1], 2.0 ** -100, None, ALU.max), dve)
                link(v.tensor_scalar(c[3].bitcast(I32), c[2].bitcast(I32), 0x7F800000, None, ALU.bitwise_and), dve)
                link(v.reciprocal(c[4], c[3]), dve)
                link(v.tensor_scalar(c[6], c[3], 2.0 ** -14 / COUNT_UNIT, None, ALU.mult), dve)
                v.tensor_scalar(c[5], c[4], 2.0 ** 14, None, ALU.mult).then_inc(s["scale_made"], 1)
                for n in range(SPLIT):
                    t = slice(n * SBT, (n + 1) * SBT)
                    dve.wait_ge(s["upper_made"], l * SPLIT + n + 1)
                    v.scalar_tensor_tensor(parts[:, t, D:P], msg[:, t, :], c[5], parts[:, t, 0:D], ALU.mult,
                                           ALU.subtract).then_inc(s["parts_made"], 1)

            def unpack(sbase, l, c, after):
                g = sbase + l * SB + after
                dve.wait_ge(counts_loaded[c % RING], (g * SLOT_LOADS[c % RING] + c // RING + 1) * 16)
                if c >= WIDE:
                    dve.wait_ge(s["counts_used"], g * (CH - 1) + c - WIDE + 1)
                elif not (isinstance(g, int) and g == 0):
                    if c == WIDE - 1:
                        dve.wait_ge(s["sums_done"], g * SBB)
                    else:
                        dve.wait_ge(s["counts_used"], g * (CH - 1))
                packed = ring[:, c % RING, :].bitcast(U16)
                v.tensor_scalar(spread[:, c % WIDE, 0, :].bitcast(U16), packed, 0x0F0F, None, ALU.bitwise_and)
                v.tensor_scalar(spread[:, c % WIDE, 1, :].bitcast(U16), packed, 4, 0x0F0F, ALU.logical_shift_right,
                                ALU.bitwise_and).then_inc(s["counts_unpacked"], 1)

            def read_sums(l, i):
                g = i + l * SB
                for b in range(SBB):
                    dve.wait_ge(s["sums_done"], g * SBB + b + 1)
                    if l and b == 0:
                        dve.wait_ge(s["h_saved"], 2 * l * SB)
                    cols = slice(b * NB, (b + 1) * NB)
                    v.scalar_tensor_tensor(zP[:, cols], ps[:, b, 0:NB], scal[:, l, 6:7],
                                           hT[:, ds(i * SBH + b // 2 * HALF + b % 2 * NB, NB)], ALU.mult,
                                           ALU.add).then_inc(s["sums_read"], 1)

            def finish(l, i, w):
                g = i + l * SB
                bank = ps[:, 6 + w, 0:7 * D].rearrange("p (k d) -> p k d", d=D)
                dve.wait_ge(s["m_done"], g * 2 + w + 1)
                if l < L - 1:
                    t = ds(i * 7 + w * HALF_T, 7)
                    v.tensor_tensor(msg[:, t, :], bank, b2row[:, l + 1:l + 2, :].to_broadcast([P, 7, D]),
                                    ALU.add).then_inc(s["m_kept"], 1)
                    dve.wait_ge(s["m_kept"], g * 2 + w + 1)
                    v.tensor_reduce(peak[:, ds(i * 2 + w, 1)], msg[:, t, :].rearrange("p k d -> p (k d)"), AX.X,
                                    ALU.max, apply_absolute_value=True).then_inc(s["peak_found"], 1)
                else:
                    t = slice(7 * w, 7 * w + 7)
                    if w == 0 and not (isinstance(i, int) and i == 0):
                        dve.wait_ge(s["out_stored"], 32 * i)
                    v.tensor_tensor(out_t[:, t, :], bank, bfrow[:].unsqueeze(1).to_broadcast([P, 7, D]),
                                    ALU.add).then_inc(s["m_kept"], 1)
                    dve.wait_ge(s["m_kept"], g * 2 + w + 1)
                    dve.wait_ge(s["x_again"], 32 * i + (48 if isinstance(i, int) and i == SB - 1 else 32))
                    v.tensor_tensor(out_t[:, t, :], out_t[:, t, :], x_t[:, t, :], ALU.add).then_inc(s["out_made"], 1)

            def stretch(l, i, first, final):
                if not first:
                    read_sums(l, i - 1)
                for c in range(1, CH):
                    unpack(i, l, c, 0)
                    if c in (8, 9) and not first:
                        finish(l, i - 1, c - 8)
                if not final:
                    unpack(i, l, 0, 1)

            dve.wait_ge(counts_stored[0], 16 * BUILD)
            dve.wait_ge(counts_stored[1], 16 * BUILD)
            dve.wait_ge(s["keys_copied"], 2 * (BUILD + 1))
            dve.wait_ge(s["overs_copied"], 2 * (BUILD + 1))
            unpack(0, 0, 0, 0)
            for l in range(L):
                scale_and_split(l, BUILD if l == 0 else 2 * SB)
                stretch(l, 0, True, False)
                if l == 0:
                    judge()
                with dve.Fori(1, SB - 1) as i:
                    stretch(l, i, False, False)
                stretch(l, SB - 1, False, l == L - 1)
                read_sums(l, SB - 1)
                finish(l, SB - 1, 0)
                finish(l, SB - 1, 1)
            dve.wait_ge(s["good_shared"], 1)
            link(v.tensor_scalar(good[:, 2:3], good[:, 2:3], float(E), None, ALU.is_equal), dve)
            link(v.tensor_scalar(good[:, 3:4], good[:, 3:4], float(P), None, ALU.is_equal), dve)
            v.tensor_tensor(good_i[:], good[0:1, 2:3], good[0:1, 3:4], ALU.mult).then_inc(s["verdict"], 1)

            def tile(l, i):
                if l == -1 and isinstance(i, int):
                    v.memset(msg[:], 0.0).then_inc(gs["zeros_made"], 1)
                pe_before = tiles_before("tensor", l, i)
                dve.wait_ge(gs["loaded"], tiles_before("loaded", l, i) + TILE_SIGNALS["loaded"][l + 1])
                if l == -1:
                    v.tensor_copy(tile_z, tile_h).then_inc(gs["vector"], 1)
                else:
                    v.tensor_tensor(tile_z, tile_h, tile_agg, ALU.add).then_inc(gs["vector"], 1)
                if 0 <= l < L - 1:
                    dve.wait_ge(gs["tensor"], pe_before + 4)
                    v.tensor_tensor(tile_hn, ps[:, 3, 0:D], b2row[:, l, :], ALU.add).then_inc(gs["vector"], 1)
                dve.wait_ge(gs["tensor"], pe_before + TILE_SIGNALS["tensor"][l + 1])
                if l < L - 1:
                    v.tensor_tensor(tile_m, ps[:, 5, 0:D], b2row[:, l + 1, :], ALU.add).then_inc(gs["vector"], 1)
                else:
                    n = TAIL if isinstance(i, int) else P
                    v.tensor_tensor(tile_m[0:n], ps[0:n, 5, 0:D], bfrow[0:n], ALU.add).then_inc(gs["vector"], 1)
                    dve.wait_ge(gs["vector"], tiles_before("vector", l, i) + 2)
                    v.tensor_tensor(tile_m[0:n], tile_m[0:n], tile_x[0:n], ALU.add).then_inc(gs["vector"], 1)

            def edges(l):
                with dve.Fori(0, EDGE_CHUNKS) as c:
                    dve.wait_ge(es[l]["src_loaded"], c * 16 + 16)
                    v.tensor_copy(e_srcf, e_src).then_inc(es[l]["vector"], 1)
                    dve.wait_ge(es[l]["vector"], c * 7 + 1)
                    v.tensor_scalar(e_diag, ident[:], e_srcf, None, ALU.mult).then_inc(es[l]["vector"], 1)
                    dve.wait_ge(es[l]["tensor"], c * 2 + 1)
                    v.tensor_scalar(e_same, ps[:, 6, 0:P], e_srcf, None, ALU.is_equal).then_inc(es[l]["vector"], 1)
                    dve.wait_ge(es[l]["vector"], c * 7 + 3)
                    dve.wait_ge(gs["below_made"], 1)
                    v.tensor_tensor(e_before, e_same, below, ALU.mult).then_inc(es[l]["vector"], 1)
                    dve.wait_ge(es[l]["vector"], c * 7 + 4)
                    v.tensor_reduce(e_seen, e_before, AX.X, ALU.add).then_inc(es[l]["vector"], 1)
                    dve.wait_ge(es[l]["vector"], c * 7 + 5)
                    v.scalar_tensor_tensor(e_to, e_seen, 65536.0, e_srcf, ALU.mult, ALU.add).then_inc(
                        es[l]["vector"], 1)
                    dve.wait_ge(es[l]["tensor"], c * 2 + 2)
                    dve.wait_ge(es[l]["sums"], c * 16 + 16)
                    v.tensor_tensor(e_agg, e_agg, ps[:, 7, 0:D], ALU.add).then_inc(es[l]["vector"], 1)

            general(dve, tile, edges)

        @block.scalar
        def _(act):
            a = nc.scalar
            act.wait_ge(s["variance_made"], 1)
            a.activation(stat[:, 2, :], stat[:, 1, :], ACT.Sqrt).then_inc(s["root_made"], 1)
            for n in range(-(-KT // 4)):
                w = min(4, KT - 4 * n) * P
                act.wait_ge(s["h0_turned"], n + 1)
                last = a.copy(hT[0:D, n * 4 * P:n * 4 * P + w], ps[0:D, 2 + n % 2, 0:w])
                last.then_inc(s["h0_kept"], 1)

            act.wait_ge(s["weights_loaded"], 16 * 8)

            def weight_overs(i, q):
                slot = q % HOTS
                if q % TB == 0:
                    wait_alone(act, s["overs_copied"], i * 2 + q // TB + 1)
                wait_alone(act, s["rows_made"], i * IB + q + 1)
                for n in range(BATCH):
                    rows = hot_r[:, slot, MAINS + n, :]
                    last = a.activation(rows, rows, ACT.Copy, scale=over_weight[:, q // TB, q % TB, n:n + 1])
                last.then_inc(s["overs_weighted"], 1)

            def keep_batch(i, q, first):
                slot = q % PSLOTS
                if q % TB == 0 and not first:
                    act.wait_ge(counts_stored[q // TB], i * 16)
                wait_alone(act, s["batch_multiplied"], i * IB + q + 1)
                g = q * 2 * BATCH
                banks = ps[:, 2 * slot:2 * slot + 2, 0:BATCH * WITH].rearrange("p k (pair n) -> p k pair n", n=WITH)
                a.activation(stage[:, g:g + 2 * BATCH, :].rearrange("p (pair k) n -> p k pair n", k=2),
                             banks[:, :, :, 0:LO], ACT.Copy)
                a.activation(row_edges[:, ds(i * IB + q, 1), :].rearrange("p a (pair k) -> p k (a pair)", k=2),
                             banks[:, :, :, LO], ACT.Copy).then_inc(s["batch_kept"], 1)

            def keep_tile(i, first):
                for q in range(IB):
                    weight_overs(i, q)
                    if q >= KEEP_LAG:
                        keep_batch(i, q - KEEP_LAG, first)
                    elif not first:
                        keep_batch(i - 1, IB + q - KEEP_LAG, True)
                    if q == 5:
                        act.wait_ge(s["hidden0_done"], i + 1)
                        if not first:
                            act.wait_ge(s["message0_done"], i)
                        a.activation(uS[:], ps[0:D, 6, 0:2 * P], ACT.Relu, bias=b1s[:, 0:1]).then_inc(
                            s["hidden0_kept"], 1)

            keep_tile(0, True)
            with act.Fori(1, BUILD) as i:
                keep_tile(i, False)
            for q in range(IB - KEEP_LAG, IB):
                keep_batch(BUILD - 1, q, True)

            def epilogue(l, i):
                g = i + l * SB
                for b in range(SBB):
                    act.wait_ge(s["u_done"], g * SBB + b + 1)
                    a.activation(U[:, b * NB:(b + 1) * NB], ps[0:D, 4 + b % 2, 0:NB], ACT.Relu,
                                 bias=b1s[:, l:l + 1]).then_inc(s["u_kept"], 1)
                for b in range(SBB):
                    act.wait_ge(s["h_done"], g * SBB + b + 1)
                    if b == 0 and l < L - 1 and not (isinstance(i, int) and g == 0):
                        act.wait_ge(s["h_saved"], 2 * g)
                    if b == 0 and l == L - 1:
                        act.wait_ge(s["h_saved"], 2 * (L - 1) * SB)
                    a.activation(hN[:, b * NB:(b + 1) * NB], ps[0:D, 4 + b % 2, 0:NB], ACT.Identity,
                                 bias=b2s[:, l:l + 1]).then_inc(s["h_kept"], 1)
                for b in range(SBB if l < L - 1 else 0):
                    act.wait_ge(s["v_done"], g * SBB + b + 1)
                    a.activation(V[:, b * NB:(b + 1) * NB], ps[0:D, 4 + b % 2, 0:NB], ACT.Relu,
                                 bias=b1s[:, l + 1:l + 2]).then_inc(s["v_kept"], 1)

            for l in range(L):
                act.wait_ge(s["scale_made"], l + 1)
                if l == 0:
                    act.wait_ge(s["message_kept"], BUILD)
                for n in range(SPLIT):
                    t = slice(n * SBT, (n + 1) * SBT)
                    a.activation(parts[:, t, 0:D], msg[:, t, :], ACT.Copy, scale=scal[:, l, 5:6]).then_inc(
                        s["upper_made"], 1)
                epilogue(l, 0)
                with act.Fori(1, SB) as i:
                    epilogue(l, i)

            def tile(l, i):
                pe_before = tiles_before("tensor", l, i)
                relu, plain = ACT.Relu, ACT.Identity
                act.wait_ge(gs["tensor"], pe_before + 1)
                a.copy(zT_g, ps[0:D, 0, 0:P]).then_inc(gs["scalar"], 1)
                if l >= 0:
                    act.wait_ge(gs["tensor"], pe_before + 2)
                    a.activation(uT_g, ps[0:D, 1, 0:P], relu, bias=b1s[:, l:l + 1]).then_inc(gs["scalar"], 1)
                    act.wait_ge(gs["tensor"], pe_before + 3)
                    a.activation(hT_g, ps[0:D, 2, 0:P], plain, bias=b2s[:, l:l + 1]).then_inc(gs["scalar"], 1)
                if l < L - 1:
                    act.wait_ge(gs["tensor"], pe_before + (2 if l == -1 else 5))
                    a.activation(vT_g, ps[0:D, 4, 0:P], relu, bias=b1s[:, l + 1:l + 2]).then_inc(gs["scalar"], 1)

            general(act, tile, None)

        @block.tensor
        def _(pe):
            t = nc.tensor
            pe.wait_ge(s["constants_made"], 6)
            pe.wait_ge(s["tops_cast"], 1)
            half = TOP // 2
            for j in range(2):
                last = t.matmul(ps[:, j, 0:half], ones[0:1, :], first_f[:, j * half:(j + 1) * half], start=True, stop=True)
            last.then_inc(s["tops_spread"], 1)
            pe.wait_ge(s["h0_made"], 1)
            for n in range(-(-KT // 4)):
                if n >= 2:
                    pe.wait_ge(s["h0_kept"], n - 1)
                for j in range(min(4, KT - 4 * n)):
                    last = t.transpose(ps[0:D, 2 + n % 2, j * P:(j + 1) * P], msg[:, 4 * n + j, :], ident[:])
                last.then_inc(s["h0_turned"], 1)
            pe.wait_ge(s["keys_made"], 1)
            for n in range(WT):
                if n >= 4:
                    pe.wait_ge(s["keys_kept"], n - 3)
                bank = ps[:, 4 + n % 4, :].bitcast(F16).rearrange("p (a g) -> p a g", a=8)
                for j, key in enumerate((row_key, col_key, weight)):
                    for k in range(2):
                        last = t.transpose(bank[:, 2 * j + k, :], key[:, n, k * P:(k + 1) * P], ident16[:])
                last.then_inc(s["keys_turned"], 1)

            pe.wait_ge(s["weights_loaded"], 16 * 8)
            pe.wait_ge(s["h0_kept"], -(-KT // 4))
            pe.wait_ge(s["keys_kept"], WT)

            def multiply_tile(i, first):
                for q in range(IB):
                    hot, slot = q % HOTS, q % PSLOTS
                    wait_alone(pe, s["hots_made"], i * IB + q + 1)
                    wait_alone(pe, s["inverses_made"], i * IB + q + 1)
                    wait_alone(pe, s["overs_weighted"], i * IB + q + 1)
                    if q >= PSLOTS:
                        wait_alone(pe, s["batch_kept"], i * IB + q - PSLOTS + 1)
                    elif not first:
                        before = max(k for k in range(IB) if k % PSLOTS == slot)
                        wait_alone(pe, s["batch_kept"], i * IB + before + 1 - IB)
                    for n in range(2 * BATCH):
                        pair, k = n // 2, n % 2
                        half = slice(k * OVER, (k + 1) * OVER)
                        over = MAINS + pair
                        prod = ps[:, 2 * slot + k, pair * WITH:pair * WITH + LO + 1]
                        t.matmul(prod, hot_r[:, hot, n, :], hot_c[:, hot, n, 0:LO + 1], start=True, stop=False)
                        last = t.matmul(prod, hot_r[half, hot, over, :], hot_c[half, hot, over, 0:LO + 1], start=False,
                                        stop=True)
                    last.then_inc(s["batch_multiplied"], 1)
                    if q == 2:
                        wait_alone(pe, s["h_copied"], i + 1)
                        if not first:
                            wait_alone(pe, s["hidden0_kept"], i)
                        t.matmul(ps[0:D, 6, 0:2 * P], W1s[0:D, 0, :], hS[:], start=True, stop=True).then_inc(
                            s["hidden0_done"], 1)
                    if q == 6:
                        wait_alone(pe, s["hidden0_kept"], i + 1)
                        if not first:
                            wait_alone(pe, s["message_kept"], i)
                        for k in range(2):
                            last = t.matmul(ps[:, 7, k * D:(k + 1) * D], uS[:, k * P:(k + 1) * P], W2s[:, 0, :],
                                            start=True, stop=True)
                        last.then_inc(s["message0_done"], 1)

            multiply_tile(0, True)
            with pe.Fori(1, BUILD) as i:
                multiply_tile(i, False)

            def mlp_stage(l, i, n):
                g = i + l * SB
                final = l == L - 1
                steps = ["u01", "u23", "h01", "h23"] + ([] if final else ["v01", "v23"]) + ["m0", "m1"]
                if n >= len(steps):
                    return
                kind, which = steps[n][0], steps[n][1:]
                if kind in "uhv":
                    frm, w, ready, done = {"u": (zP, W1s[:, l, :], "sums_read", "u_done"),
                                           "h": (U, W2s[:, l, :], "u_kept", "h_done"),
                                           "v": (hN, None if final else W1s[0:D, l + 1, :], "h_kept", "v_done")}[kind]
                    for b in (int(c) for c in which):
                        wait_alone(pe, s[ready], g * SBB + b + 1)
                        if kind == "u" and b >= 2:
                            wait_alone(pe, s["u_kept"], g * SBB + b - 1)
                        if kind == "h" and b < 2:
                            wait_alone(pe, s["u_kept"], g * SBB + b + 3)
                        if kind == "h" and b >= 2:
                            wait_alone(pe, s["h_kept"], g * SBB + b - 1)
                        if kind == "v" and b < 2:
                            wait_alone(pe, s["h_kept"], g * SBB + b + 3)
                        if kind == "v" and b >= 2:
                            wait_alone(pe, s["v_kept"], g * SBB + b - 1)
                        t.matmul(ps[0:D, 4 + b % 2, 0:NB], w, frm[:, b * NB:(b + 1) * NB], start=True, stop=True).then_inc(
                            s[done], 1)
                else:
                    w = int(which)
                    if final:
                        frm, weights = hN, Wfs[:]
                        pe.wait_ge(s["h_kept"], (g + 1) * SBB)
                    else:
                        frm, weights = V, W2s[:, l + 1, :]
                        pe.wait_ge(s["v_kept"], (g + 1) * SBB)
                    for k in range(7):
                        c = (7 * w + k) * P
                        last = t.matmul(ps[:, 6 + w, k * D:(k + 1) * D], frm[:, c:c + P], weights, start=True, stop=True)
                    last.then_inc(s["m_done"], 1)

            def multiply_stretch(l, i, first):
                g = i + l * SB
                for c in range(CH):
                    wait_alone(pe, s["counts_unpacked"], g * CH + c + 1)
                    for k in range(c * CK, (c + 1) * CK):
                        if first and k % SBT == 0:
                            pe.wait_ge(s["parts_made"], l * SPLIT + k // SBT + 1)
                        for b in range(SBB):
                            if k == 0 and not (isinstance(i, int) and g == 0):
                                wait_alone(pe, s["sums_read"], g * SBB + b + 1 - SBB)
                            at = (k % CK) * SBH + b % 2 * NB
                            last = t.matmul(ps[:, b, 0:NB], parts[:, k, :], spread[:, c % WIDE, b // 2, at:at + NB].bitcast(F8), start=k == 0,
                                            stop=k == KT - 1)
                            if k == KT - 1:
                                last.then_inc(s["sums_done"], 1)
                    if c < CH - 1:
                        last.then_inc(s["counts_used"], 1)
                    if not first:
                        mlp_stage(l, i - 1, c)

            for l in range(L):
                multiply_stretch(l, 0, True)
                with pe.Fori(1, SB) as i:
                    multiply_stretch(l, i, False)
                for n in range(8):
                    mlp_stage(l, SB - 1, n)

            def tile(l, i):
                act_before = tiles_before("scalar", l, i)
                wait_alone(pe, gs["vector"], tiles_before("vector", l, i) + 1)
                t.transpose(ps[0:D, 0, 0:P], tile_z, ident[:]).then_inc(gs["tensor"], 1)
                wait_alone(pe, gs["scalar"], act_before + 1)
                h = zT_g
                if l >= 0:
                    t.matmul(ps[0:D, 1, 0:P], W1s[0:D, l, :], zT_g, start=True, stop=True).then_inc(gs["tensor"], 1)
                    wait_alone(pe, gs["scalar"], act_before + 2)
                    t.matmul(ps[0:D, 2, 0:P], W2s[:, l, :], uT_g, start=True, stop=True).then_inc(gs["tensor"], 1)
                    if l < L - 1:
                        t.matmul(ps[:, 3, 0:D], uT_g, W2s[:, l, :], start=True, stop=True).then_inc(gs["tensor"], 1)
                    wait_alone(pe, gs["scalar"], act_before + 3)
                    h = hT_g
                if l < L - 1:
                    t.matmul(ps[0:D, 4, 0:P], W1s[0:D, l + 1, :], h, start=True, stop=True).then_inc(gs["tensor"], 1)
                    wait_alone(pe, gs["scalar"], act_before + TILE_SIGNALS["scalar"][l + 1])
                    t.matmul(ps[:, 5, 0:D], vT_g, W2s[:, l + 1, :], start=True, stop=True).then_inc(gs["tensor"], 1)
                else:
                    t.matmul(ps[:, 5, 0:D], h, Wfs[:], start=True, stop=True).then_inc(gs["tensor"], 1)

            def edges(l):
                with pe.Fori(0, EDGE_CHUNKS) as c:
                    wait_alone(pe, es[l]["vector"], c * 7 + 2)
                    t.matmul(ps[:, 6, 0:P], ones[:], e_diag, start=True, stop=True).then_inc(es[l]["tensor"], 1)
                    wait_alone(pe, es[l]["vector"], c * 7 + 3)
                    wait_alone(pe, es[l]["messages"], c * 16 + 16)
                    t.matmul(ps[:, 7, 0:D], e_same, e_msg, start=True, stop=True).then_inc(es[l]["tensor"], 1)

            general(pe, tile, edges)


_INS = ["x", "src", "dst", "L0_gnn_W1", "L0_gnn_b1", "L0_gnn_W2", "L0_gnn_b2", "L0_gnn_Wf", "L0_gnn_bf"]


def kernel(**inputs):
    import numpy as _np
    import concourse.bacc as _bacc
    from concourse import mybir as _mybir
    from concourse.bass_utils import run_bass_kernel_spmd as _run

    nc = _bacc.Bacc("TRN2", target_bir_lowering=False, num_devices=1)
    arrays, args = {}, []
    for name in _INS:
        a = _np.ascontiguousarray(inputs[name])
        arrays[f"in_{name}_dram"] = a
        args.append(nc.dram_tensor(f"in_{name}_dram", a.shape, _mybir.dt.from_np(a.dtype), kind="ExternalInput").ap())
    args.append(nc.dram_tensor("out_dram", (N, D), _mybir.dt.float32, kind="ExternalOutput").ap())
    gnn_kernel(nc, *args)
    r = _run(nc, [arrays], core_ids=[0])
    return r.results[0]["out_dram"]
```

```python
from contextlib import ExitStack

import numpy as np
import concourse.bass as bass
from concourse import mybir
from concourse.alu_op_type import AluOpType as ALU

F32, F16, F8 = mybir.dt.float32, mybir.dt.float16, mybir.dt.float8e4
I32, U16, U8 = mybir.dt.int32, mybir.dt.uint16, mybir.dt.uint8
ACT = mybir.ActivationFunctionType
AX = mybir.AxisListType
ds = bass.ds

P = 128
N, D, L, E = 12500, 64, 3, 400000
KT = -(-N // P)
NP = KT * P
TAIL = N - (KT - 1) * P

GN = 4
HALF = NP // 2
HALF_T = KT // 2
HI = P // GN
LO = HALF // HI
TG = P // GN
MAIN, OVER = 128, 64
WIN = MAIN + OVER
GRAN = 16
ROWS = E // GRAN
FAN = 128
TOP = -(-ROWS // FAN)
LAST_START = ROWS - WIN // GRAN
WT = -(-KT * TG // P)
KG = 5
PAIRS = TG // 2
TRIO = 3
WAVE = 4
MAINS = 2 * WAVE
WKEYS = WAVE * TRIO
BATCH = 2
KINDS = 3
KEYS = KINDS * PAIRS * TRIO
NIBBLE = 16
COUNT_UNIT = 2.0 ** -9
LO_BITS = 9
PK = 100
PC = E // PK
ROUND = 12582912.0
BIG = 1 << 24

HOTS = 4
PSLOTS = 3
BUILD = KT // 2
TB = PAIRS // BATCH
IB = 2 * TB
TW = PAIRS // WAVE
IW = 2 * TW
WB = WAVE // BATCH
KEEP_LAG = 2
WITH = LO + 2

NB = 448
SBB = 4
SBC = NB * SBB
SBH = SBC // 2
SBT = SBC // P
SB = NP // SBC
CK = 7
CH = KT // CK
RING = 4
FINISH = [(0, 4), (4, 3)]
WIDE = 2
SLOT_LOADS = [len(range(s, CH, RING)) for s in range(RING)]
ORDER = [c for c in range(CH) if c % SB < SB - 1] + [SB - 1, CH - 1]
EARLY = CH - 2
EARLY_PEAKS = 2 * (SB - 1)
SCALED = 2.0 ** 10
SCALED_LIMIT = 2.0 ** 15
EPS = 1e-5
LN_SUM_TO_MEAN = 1.0 / D


def gnn_kernel(nc, x, src, dst, W1, b1, W2, b2, Wf, bf, out):
    ctx = ExitStack()
    with ctx:
        def sb(name, shape, dt):
            return ctx.enter_context(nc.sbuf_tensor(name, shape, dt))

        def sem(name):
            return ctx.enter_context(nc.semaphore(name))

        def scratch(name, shape, dt):
            return nc.dram_tensor(name, shape, dt, kind="Internal").ap()

        counts_dram = scratch("counts_dram", (KT, TG, P, LO), U8)
        firsts_dram = scratch("firsts_dram", (TOP * FAN,), I32)
        packed_dram = scratch("packed_dram", (E,), I32)
        h0_dram = scratch("h0_dram", (NP, D), F32)
        h_dram = scratch("h_dram", (NP, D), F32)
        m_dram = scratch("m_dram", (NP, D), F32)
        agg_dram = scratch("agg_dram", (NP, D), F32)
        counts_rows = counts_dram.rearrange("k g p n -> (k g p n)").rearrange(
            "(c k r s) -> c r k s", k=CK, r=P, s=HALF)

        hT = sb("hT", [P, HALF], F32)
        msg = sb("msg", [P, KT, D], F32)
        parts = sb("parts", [P, KT, P], F16)
        W1s = sb("W1s", [P, L, D], F32)
        W2s = sb("W2s", [D, L, D], F32)
        Wfs = sb("Wfs", [D, D], F32)
        W1b = sb("W1b", [P, L, P], F32)
        W2b = sb("W2b", [P, L, P], F32)
        Wfb = sb("Wfb", [P, P], F32)
        b1s = sb("b1s", [P, L], F32)
        b2s = sb("b2s", [P, L], F32)
        b2row = sb("b2row", [P, L, D], F32)
        bfrow = sb("bfrow", [P, D], F32)
        ident = sb("ident", [P, P], F32)
        ident16 = sb("ident16", [P, P], F16)
        ones = sb("ones", [P, P], F32)
        ones16 = sb("ones16", [P, 2], F16)
        iota = sb("iota", [P, LO], F16)
        node_i = sb("node_i", [P, WT], I32)
        node = sb("node", [P, WT], F32)
        node_hi = sb("node_hi", [P, WT], F32)
        cnt = sb("cnt", [P, WT], F32)
        row = sb("row", [P, WT], F32)
        row_i = sb("row_i", [P, WT], I32)
        start_i = sb("start_i", [P, WT], I32)
        stat = sb("stat", [P, 4, KT], F32)
        peak = sb("peak", [P, BUILD], F32)
        scal = sb("scal", [P, L, 8], F32)
        good = sb("good", [P, 4], F32)
        fits = sb("fits", [P, L, 2], F32)
        good_i = sb("good_i", [1, 1], I32)
        pad_i = sb("pad_i", [1, TOP * FAN - ROWS], I32)

        ARENA = 95232
        arena = sb("arena", [P, ARENA], U8)

        def view(at, shape, dt, rows=P):
            size = {F32: 4, I32: 4, F16: 2, U8: 1}[dt]
            n = size * int(np.prod(shape))
            assert at % 4 == 0 and at + n <= ARENA
            v = arena[0:rows, at:at + n].bitcast(dt)
            if len(shape) == 2:
                v = v.rearrange("p (a b) -> p a b", a=shape[0])
            if len(shape) == 3:
                v = v.rearrange("p (a b c) -> p a b c", a=shape[0], b=shape[1])
            return v, at + n

        dst_t, at = view(0, [PC], I32, PK)
        src_t, at = view(at, [PC], I32, PK)
        pa, at = view(at, [PC], F32, PK)
        pb, at = view(at, [PC], F32, PK)
        pc, at = view(at, [PC], I32, PK)
        firsts, at = view(at, [ROWS // PK], I32, PK)
        first_i, at = view(at, [TOP], I32, 1)
        first_f, at = view(at, [TOP], F32, 1)
        keys, at = view(0, [KINDS, 4 * WT, KEYS // KINDS], F16)
        win, end = view(at, [WT, WIN], I32)
        win_row, end = view(end, [KG, WIN], I32)
        win_rowf = win_row.bitcast(F32)
        fan = hT[:, 0:WT * FAN].bitcast(I32).rearrange("p (t f) -> p t f", f=FAN)
        compare = hT[:, 0:WT * TOP].rearrange("p (t f) -> p t f", f=TOP)
        compare_fan = parts[:].rearrange("p k c -> p (k c)").bitcast(F32)[:, 0:WT * FAN].rearrange(
            "p (t f) -> p t f", f=FAN)
        col_key, end = view(ARENA - 2 * KINDS * WT * 2 * P, [WT, 2 * P], F16)
        row_key, end = view(end, [WT, 2 * P], F16)
        weight, end = view(end, [WT, 2 * P], F16)
        assert end <= ARENA
        hot_c, at = view(at, [HOTS, WKEYS, WITH], F16)
        hot_r, at = view(at, [HOTS, WKEYS, P], F16)
        stage, at = view(at, [2 * TG, LO], U8)
        key_now = sb("key_now", [P, 2, KEYS, 2], F16)
        over_weight = sb("over_weight", [P, 2, TW, WAVE], F32)
        hS = sb("hS", [P, P], F32)
        uS = sb("uS", [P, P], F32)
        row_edges, _ = view(ARENA - 2 * BUILD * IB * 2 * BATCH, [BUILD * IB, 2 * BATCH], F16)
        ring, at = view(0, [RING, CK * SBH], U8)
        spread, at = view(at, [WIDE, 2, CK * SBH], U8)
        zP, at = view(at, [SBC], F32)
        U, at = view(at, [SBH], F32)
        hN, at = view(at, [SBH], F32)
        V, at = view(at, [SBH], F32)
        x_t, at = view(at, [SBT, D], F32)
        out_t, at = view(at, [SBT, D], F32)
        tile_h, at = view(0, [D], F32)
        tile_agg, at = view(at, [D], F32)
        tile_x, at = view(at, [D], F32)
        tile_z, at = view(at, [D], F32)
        tile_hn, at = view(at, [D], F32)
        tile_m, at = view(at, [D], F32)
        zT_g, at = view(at, [P], F32, D)
        uT_g, at = view(at, [P], F32, D)
        hT_g, at = view(at, [P], F32, D)
        vT_g, at = view(at, [P], F32, D)
        e_dst, at = view(at, [1], I32)
        e_src, at = view(at, [1], I32)
        e_to, at = view(at, [1], I32)
        e_srcf, at = view(at, [1], F32)
        e_seen, at = view(at, [1], F32)
        e_msg, at = view(at, [D], F32)
        e_agg, at = view(at, [D], F32)
        e_diag, at = view(at, [P], F32)
        e_same, at = view(at, [P], F32)
        e_before, at = view(at, [P], F32)
        below, at = view(at, [P], F32)

        ps = ctx.enter_context(nc.psum_tensor("ps", [P, 8, 512], F32))

        s = {n: sem(n) for n in (
            "dst_loaded", "src_loaded", "x_loaded", "weights_loaded", "blocks_cleared", "constants_made", "pad_made", "x_padded",
            "firsts_made", "firsts_stored", "tops_loaded", "tops_cast", "tops_spread",
            "packed_made", "packed_stored", "rows_found", "fans_gathered", "starts_found", 
            "vector_chain", "variance_made", "root_made", "h0_made", "h0_stored", "h0_turned", "h0_kept",
            "quotients_made", "x_centred", "squares_made", "columns_found", "columns_kept",
            "keys_made", "keys_turned", "mains_kept", "overs_kept", "keys_copied", "overs_copied", "rows_made", "hots_made", "overs_weighted", "inverses_made", "batch_multiplied", "batch_kept",
            "counts_stored_0", "counts_stored_1",
            "h_copied", "hidden0_done", "hidden0_kept", "message0_done", "message_kept",
            "peak_found", "peak_made", "peak_shared", "scale_made", "upper_made", "parts_made",
            "counts_unpacked", "counts_used", "sums_done", "sums_read", "u_done", "u_kept", "h_done", "h_kept", "h_saved",
            "v_done", "v_kept", "m_done", "m_kept", "x_again", "out_done", "out_made", "out_read", "out_stored",
            "good_made", "good_shared", "verdict",
        )}
        gs = {n: sem("general_" + n) for n in (
            "tensor", "scalar", "vector", "loaded", "stored", "zeros_made", "agg_cleared", "below_made")}
        es = [{n: sem(f"edges_{n}_{l}") for n in (
            "dst_loaded", "src_loaded", "messages", "sums", "vector", "tensor", "added")} for l in range(L)]
        windows_gathered = [sem(f"windows_gathered_{n}") for n in range(WT // KG)]
        counts_loaded = [sem(f"counts_loaded_{r}") for r in range(RING)]
        counts_stored = [s["counts_stored_0"], s["counts_stored_1"]]

        chain = [0]

        def link(ins, eng):
            chain[0] += 1
            ins.then_inc(s["vector_chain"], 1)
            eng.wait_ge(s["vector_chain"], chain[0])

        passed = {e: sem(f"waits_passed_{e}") for e in ("sync", "scalar", "tensor", "gpsimd")}


        def wait_alone(eng, semaphore, value):
            eng.wait_ge(semaphore, value)
            if not isinstance(value, int):
                eng.sem_inc(passed[{"SP": "sync", "Activation": "scalar", "PE": "tensor", "Pool": "gpsimd"}[eng.engine.name]], 1)

        TILE_SIGNALS = {"tensor": [3] + [6] * (L - 1) + [4], "scalar": [2] + [4] * (L - 1) + [3],
                        "vector": [2] + [3] * (L - 1) + [3], "loaded": [16] + [32] * (L - 1) + [48],
                        "stored": [16] + [32] * (L - 1) + [16]}
        EDGE_CHUNKS = E // P
        TURNS = -(-HALF_T // 4)
        WEIGHT_LOADS = 16

        def tiles_before(kind, l, t):
            each = TILE_SIGNALS[kind]
            return t * each[l + 1] + KT * sum(each[:l + 1])

        def general(eng, tile, edges):
            eng.wait_ge(s["verdict"], 1)
            fine = eng.value_load(good_i[0:1, 0:1], min_val=0, max_val=1)
            with eng.If(fine < 1):
                for l in range(-1, L):
                    if tile is not None:
                        with eng.Fori(0, KT - 1) as i:
                            tile(l, i)
                        tile(l, KT - 1)
                    if edges is not None and l < L - 1:
                        edges(l + 1)

        halves = msg[:].rearrange("p (w k) d -> p k w d", w=2)

        stacked_h0 = parts[:].rearrange("p k c -> p (k c)").bitcast(F32).rearrange("p (k w d) -> p k w d", w=2, d=D)

        def key_bank(n):
            at = (0, 4, 6)[n % 3]
            banks = ps[:, at:at + 2, :].rearrange("p two n -> p (two n)").bitcast(F16).rearrange(
                "p (two n) -> p two n", two=2)
            return banks[:, :, 0:KINDS * P].rearrange("p two (j g) -> p two j g", g=P)

        def key_rows(n):
            return keys[:, :, 4 * n:4 * n + 4, :].rearrange("p j k (b c) -> p j (k b) c", c=WKEYS)

        block = ctx.enter_context(nc.Block())

        @block.sync
        def _(sp):
            sp.dma_start(dst_t, dst.rearrange("(p c) -> p c", p=PK)).then_inc(s["dst_loaded"], 16)
            sp.dma_start(src_t, src.rearrange("(p c) -> p c", p=PK)).then_inc(s["src_loaded"], 16)
            weights = [(W1s[0:D], W1.rearrange("l k m -> k l m")), (W1s[D:P], W1.rearrange("l k m -> k l m")),
                       (W2s[:], W2.rearrange("l k m -> k l m")), (Wfs[:], Wf),
                       (b2row[:], b2.rearrange("l d -> (l d)").partition_broadcast(P)), (bfrow[:], bf.partition_broadcast(P))]
            for r in (slice(0, D), slice(D, P)):
                weights += [(W1b[r, :, r], W1.rearrange("l k m -> k l m")), (W2b[r, :, r], W2.rearrange("l k m -> k l m")),
                            (Wfb[r, r], Wf), (b1s[r], b1.rearrange("l d -> d l")), (b2s[r], b2.rearrange("l d -> d l"))]
            assert len(weights) == WEIGHT_LOADS
            sp.wait_ge(s["blocks_cleared"], 3)
            for to, frm in weights:
                if to.ndim == 3 and to.shape[0] == P and frm.ndim == 2:
                    to = to.rearrange("p l d -> p (l d)")
                with nc.allow_non_contiguous_dma(reason="192 biases"):
                    sp.dma_start(to, frm).then_inc(s["weights_loaded"], 16)
            sp.wait_ge(s["firsts_made"], 1)
            sp.wait_ge(s["pad_made"], 1)
            sp.dma_start(firsts_dram[0:ROWS].rearrange("(p c) -> p c", p=PK), firsts).then_inc(s["firsts_stored"], 16)
            sp.dma_start(firsts_dram[ROWS:].rearrange("(p c) -> p c", p=1), pad_i[:]).then_inc(s["firsts_stored"], 16)
            sp.wait_ge(s["firsts_stored"], 32)
            with nc.allow_non_contiguous_dma(reason="one number of each row"):
                sp.dma_start(first_i, firsts_dram.rearrange("(p r f) -> p r f", p=1, f=FAN)[:, :, 0]).then_inc(
                    s["tops_loaded"], 16)
            sp.wait_ge(s["packed_made"], 1)
            sp.dma_start(packed_dram.rearrange("(p c) -> p c", p=PK), pc).then_inc(s["packed_stored"], 16)
            sp.wait_ge(s["h0_made"], 2)
            for w in range(2):
                sp.dma_start(h0_dram[w * HALF:(w + 1) * HALF, :].rearrange("(k p) d -> p k d", p=P),
                             stacked_h0[:, :, w, :]).then_inc(s["h0_stored"], 16)

            with sp.Fori(0, BUILD) as i:
                for u in range(2):
                    wait_alone(sp, s["batch_kept"], i * IB + (u + 1) * TB)
                    sp.dma_start(counts_dram[ds(i * 2 + u, 1)].rearrange("k g p n -> p (k g) n"),
                                 stage[:, u * TG:(u + 1) * TG, :]).then_inc(counts_stored[u], 16)

            sp.wait_ge(counts_stored[0], 16 * BUILD)
            sp.wait_ge(counts_stored[1], 16 * BUILD)
            sp.wait_ge(s["keys_copied"], 2 * (BUILD + 1))
            sp.wait_ge(s["overs_copied"], 2 * (BUILD + 1))

            def load_stretch(sbase, l, first):
                g = sbase + l * SB
                for c in range(CH):
                    r = c % RING
                    if c >= RING:
                        wait_alone(sp, s["counts_unpacked"], g * CH + (c - RING + 1))
                    elif not first:
                        before = max(k for k in range(CH) if k % RING == r)
                        wait_alone(sp, s["counts_unpacked"], g * CH + (before + 1 - CH))
                    sp.dma_start(ring[:, r, :].rearrange("p (k n) -> p k n", k=CK),
                                 counts_rows[ORDER[c]][:, :, ds(sbase * SBH, SBH)]).then_inc(counts_loaded[r], 16)

            def load_x(sbase):
                for w in range(2):
                    sp.dma_start(x_t[:, 7 * w:7 * w + 7, :],
                                 x[ds((sbase - 1) * SBH + w * HALF, SBH), :].rearrange("(k p) d -> p k d", p=P)).then_inc(
                        s["x_again"], 16)

            for l in range(L):
                load_stretch(0, l, l == 0)
                with sp.Fori(1, SB) as i:
                    if l == L - 1:
                        load_x(i)
                    load_stretch(i, l, False)
                    if l == L - 1:
                        wait_alone(sp, s["out_made"], 2 * i)
                        for w in range(2):
                            sp.dma_start(out[ds((i - 1) * SBH + w * HALF, SBH), :].rearrange("(k p) d -> p k d", p=P),
                                         out_t[:, 7 * w:7 * w + 7, :]).then_inc(s["out_stored"], 16)
            sp.wait_ge(s["out_made"], 2 * (SB - 1))
            last = (SB - 1) * SBH
            pieces = [(slice(0, 7), last, P), (slice(7, SBT - 1), last + HALF, P), (slice(SBT - 1, SBT), (KT - 1) * P, TAIL)]
            for t, at, n in pieces:
                rows = (t.stop - t.start - 1) * P + n
                sp.dma_start(x_t[0:n, t, :], x[at:at + rows, :].rearrange("(k p) d -> p k d", p=n)).then_inc(
                    s["x_again"], 16)
            sp.wait_ge(s["out_made"], 2 * SB)
            for t, at, n in pieces:
                rows = (t.stop - t.start - 1) * P + n
                sp.dma_start(out[at:at + rows, :].rearrange("(k p) d -> p k d", p=n), out_t[0:n, t, :]).then_inc(
                    s["out_stored"], 16)
            sp.wait_ge(s["out_stored"], 16 * (2 * (SB - 1) + 3))
            sp.wait_ge(s["h0_stored"], 32)

            def tile(l, i):
                rows = ds(i * P, P)
                n = TAIL if isinstance(i, int) else P
                sp.dma_start(tile_h, (h0_dram if l <= 0 else h_dram)[rows, :]).then_inc(gs["loaded"], 16)
                if l >= 0:
                    sp.dma_start(tile_agg, agg_dram[rows, :]).then_inc(gs["loaded"], 16)
                if l == L - 1:
                    sp.dma_start(tile_x[0:n], x[ds(i * P, n), :]).then_inc(gs["loaded"], 16)
                before = tiles_before("vector", l, i)
                if 0 <= l < L - 1:
                    wait_alone(sp, gs["vector"], before + 2)
                    sp.dma_start(h_dram[rows, :], tile_hn).then_inc(gs["stored"], 16)
                wait_alone(sp, gs["vector"], before + TILE_SIGNALS["vector"][l + 1])
                if l < L - 1:
                    sp.dma_start(m_dram[rows, :], tile_m).then_inc(gs["stored"], 16)
                else:
                    sp.dma_start(out[ds(i * P, n), :], tile_m[0:n]).then_inc(gs["stored"], 16)
                wait_alone(sp, gs["stored"], tiles_before("stored", l, i) + TILE_SIGNALS["stored"][l + 1])

            def edges(l):
                sp.wait_ge(gs["stored"], tiles_before("stored", l, 0))
                sp.wait_ge(gs["zeros_made"], 1)
                sp.dma_start(agg_dram.rearrange("(k p) d -> p k d", p=P), msg[:]).then_inc(gs["agg_cleared"], 16)
                sp.wait_ge(gs["agg_cleared"], 16 * (l + 1))
                with sp.Fori(0, EDGE_CHUNKS) as c:
                    sp.dma_start(e_dst, dst[ds(c * P, P)].unsqueeze(1)).then_inc(es[l]["dst_loaded"], 16)
                    sp.dma_start(e_src, src[ds(c * P, P)].unsqueeze(1)).then_inc(es[l]["src_loaded"], 16)
                    wait_alone(sp, es[l]["added"], c * 16 + 16)

            general(sp, tile, edges)

        @block.gpsimd
        def _(pool):
            for blocks in (W1b, W2b, Wfb):
                nc.gpsimd.memset(blocks[:], 0.0).then_inc(s["blocks_cleared"], 1)
            nc.gpsimd.memset(pad_i[:], BIG).then_inc(s["pad_made"], 1)
            nc.gpsimd.memset(ones16[:], 1.0).then_inc(s["constants_made"], 1)
            nc.gpsimd.memset(ones[:], 1.0).then_inc(s["constants_made"], 1)
            nc.gpsimd.iota(iota[:], pattern=[[1, LO]], base=0, channel_multiplier=0,
                           allow_small_or_imprecise_dtypes=True).then_inc(s["constants_made"], 1)
            nc.gpsimd.iota(node_i[:], pattern=[[GN * P, WT]], base=0, channel_multiplier=GN).then_inc(
                s["constants_made"], 1)
            pool.wait_ge(s["constants_made"], 4)
            nc.gpsimd.affine_select(out=ident[:], in_=ones[:], compare_op=ALU.is_equal, fill=0.0, base=0,
                                    pattern=[[-1, P]], channel_multiplier=1).then_inc(s["constants_made"], 1)
            pool.wait_ge(s["constants_made"], 5)
            nc.gpsimd.tensor_copy(ident16[:], ident[:]).then_inc(s["constants_made"], 1)
            pool.wait_ge(s["constants_made"], 6)
            pool.wait_ge(s["tops_loaded"], 16)
            nc.gpsimd.memset(msg[:, KT - 1, :], 0.0).then_inc(s["x_padded"], 1)
            pool.wait_ge(s["x_padded"], 1)
            pool.dma_start(msg[:, 0:KT - 1, :], x[0:(KT - 1) * P, :].rearrange("(k p) d -> p k d", p=P)).then_inc(
                s["x_loaded"], 16)
            pool.dma_start(msg[0:TAIL, KT - 1, :], x[(KT - 1) * P:N, :]).then_inc(s["x_loaded"], 16)

            pool.wait_ge(s["rows_found"], 1)
            pool.wait_ge(s["firsts_stored"], 32)
            for t in range(WT):
                pool.indirect_dma_start(fan[:, t, :], None, firsts_dram.rearrange("(r f) -> r f", f=FAN),
                                        bass.IndirectOffsetOnAxis(ap=row_i[:, t:t + 1], axis=0)).then_inc(
                    s["fans_gathered"], 16)
            pool.wait_ge(s["starts_found"], 1)
            pool.wait_ge(s["packed_stored"], 16)
            for t in range(WT):
                pool.indirect_dma_start(win[:, t, :], None, packed_dram.rearrange("(r f) -> r f", f=GRAN),
                                        bass.IndirectOffsetOnAxis(ap=start_i[:, t:t + 1], axis=0)).then_inc(
                    windows_gathered[t // KG], 16)

            pool.wait_ge(s["h0_kept"], TURNS)
            pool.wait_ge(s["mains_kept"], WT)
            pool.wait_ge(s["overs_kept"], WT)

            def copy_keys(i, u, first):
                if not first:
                    pool.wait_ge(s["hots_made"], ((i - 1) * 2 + u + 1) * TW)
                tile_keys = keys[:, :, ds(i * 2 + u, 1), :].rearrange("p j a k -> p j (a k)")
                nc.gpsimd.tensor_copy(
                    key_now[:, u, :, :].rearrange("p (j k) two -> p j k two", j=KINDS),
                    tile_keys.unsqueeze(3).to_broadcast([P, KINDS, KEYS // KINDS, 2])).then_inc(
                    s["keys_copied"], 1)
                if not first:
                    pool.wait_ge(s["overs_weighted"], ((i - 1) * 2 + u + 1) * TB)
                weights = tile_keys[:, 2, :].rearrange("p (b c) -> p b c", c=WKEYS)[:, :, MAINS:WKEYS]
                nc.gpsimd.tensor_copy(over_weight[:, u, :, :], weights).then_inc(s["overs_copied"], 1)

            def prepare(i, first):
                if not first:
                    pool.wait_ge(s["hidden0_done"], i)
                nc.gpsimd.tensor_copy(hS[:], hT[:, ds(i * P, P)]).then_inc(s["h_copied"], 1)
                for q in range(IW):
                    u, slot = q // TW, q % HOTS
                    if q % TW == 0:
                        wait_alone(pool, s["keys_copied"], i * 2 + u + 1)
                    if not first or q >= HOTS:
                        wait_alone(pool, s["batch_multiplied"], i * IB + (q - HOTS + 1) * WB)
                    k = (2 * TW + q % TW) * WKEYS
                    nc.gpsimd.tensor_scalar(hot_c[:, slot, :, LO], key_now[:, u, k:k + WKEYS, 0], -1.0 / NIBBLE,
                                            1.0 + 1.0 / NIBBLE, ALU.mult, ALU.add).then_inc(s["inverses_made"], 1)
                    if q % TW == TW - 1:
                        pool.wait_ge(s["inverses_made"], i * IW + q + 1)
                        copy_keys(i + 1, u, False)

            copy_keys(0, 0, True)
            copy_keys(0, 1, True)
            prepare(0, True)
            with pool.Fori(1, BUILD) as i:
                prepare(i, False)

            def share_peak(l):
                pool.wait_ge(s["peak_made"], l + 1)
                nc.gpsimd.partition_all_reduce(scal[:, l, 1:2], scal[:, l, 0:1], P, bass.bass_isa.ReduceOp.max).then_inc(
                    s["peak_shared"], 1)

            def save_h(l, i):
                pool.wait_ge(s["h_kept"], (i + l * SB) * 2 + 2)
                nc.gpsimd.tensor_copy(hT[:, ds(i * SBH, SBH)], hN).then_inc(s["h_saved"], 1)

            share_peak(0)
            for l in range(L - 1):
                with pool.Fori(0, SB - 1) as i:
                    save_h(l, i)
                share_peak(l + 1)
                save_h(l, SB - 1)
            pool.wait_ge(s["good_made"], 1)
            nc.gpsimd.partition_all_reduce(good[:, 2:4], good[:, 0:2], P, bass.bass_isa.ReduceOp.add).then_inc(
                s["good_shared"], 1)

            def edges(l):
                if l == 0:
                    nc.gpsimd.affine_select(out=below, in_=ones[:], compare_op=ALU.is_gt, fill=0.0, base=0,
                                            pattern=[[-1, P]], channel_multiplier=1).then_inc(gs["below_made"], 1)
                with pool.Fori(0, EDGE_CHUNKS) as c:
                    wait_alone(pool, es[l]["dst_loaded"], c * 16 + 16)
                    pool.indirect_dma_start(e_msg, None, m_dram, bass.IndirectOffsetOnAxis(ap=e_dst, axis=0)).then_inc(
                        es[l]["messages"], 16)
                    wait_alone(pool, es[l]["src_loaded"], c * 16 + 16)
                    pool.indirect_dma_start(e_agg, None, agg_dram, bass.IndirectOffsetOnAxis(ap=e_src, axis=0)).then_inc(
                        es[l]["sums"], 16)
                    wait_alone(pool, es[l]["vector"], c * 7 + 7)
                    pool.indirect_dma_start(agg_dram, bass.IndirectOffsetOnAxis(ap=e_to, axis=0), e_agg, None,
                                            bounds_check=NP - 1, oob_is_err=False).then_inc(es[l]["added"], 16)

            general(pool, None, edges)

        @block.vector
        def _(dve):
            v = nc.vector
            dve.wait_ge(s["dst_loaded"], 16)
            v.tensor_copy(firsts, dst_t.rearrange("p (c g) -> p c g", g=GRAN)[:, :, 0]).then_inc(s["firsts_made"], 1)
            dve.wait_ge(s["constants_made"], 4)
            link(v.tensor_copy(node[:], node_i[:]), dve)
            link(v.tensor_scalar(node_hi[:], node[:], float(HI), None, ALU.mult), dve)
            dve.wait_ge(s["tops_loaded"], 16)
            v.tensor_copy(first_f, first_i).then_inc(s["tops_cast"], 1)
            dve.wait_ge(s["tops_spread"], 1)
            shape = [P, WT, TOP]
            link(v.tensor_tensor(compare, ps[:, 0, 0:TOP].unsqueeze(1).to_broadcast(shape),
                                 node[:].unsqueeze(2).to_broadcast(shape), ALU.is_lt), dve)
            link(v.tensor_reduce(cnt[:], compare, AX.X, ALU.add), dve)
            link(v.tensor_scalar(row[:], cnt[:], -1.0, 0.0, ALU.add, ALU.max), dve)
            v.tensor_copy(row_i[:], row[:]).then_inc(s["rows_found"], 1)

            dve.wait_ge(s["quotients_made"], 1)
            link(v.tensor_scalar(pb, pa, ROUND, ROUND, ALU.add, ALU.subtract), dve)
            link(v.scalar_tensor_tensor(pc, pb, -float(LO), src_t, ALU.mult, ALU.add), dve)
            link(v.tensor_scalar(pa, src_t, float(HALF), HI - 0.5, ALU.is_ge, ALU.mult), dve)
            link(v.tensor_tensor(pb, pb, pa, ALU.subtract), dve)
            link(v.scalar_tensor_tensor(pa, dst_t, float(HI), pb, ALU.mult, ALU.add), dve)
            link(v.tensor_scalar(dst_t, pa, float(1 << LO_BITS), None, ALU.mult), dve)
            v.tensor_tensor(pc, dst_t, pc, ALU.bitwise_or).then_inc(s["packed_made"], 1)

            dve.wait_ge(s["fans_gathered"], 16 * WT)
            nodes = node[:].unsqueeze(2).to_broadcast([P, WT, FAN])
            link(v.tensor_tensor(compare_fan, fan, nodes, ALU.is_lt), dve)
            link(v.tensor_reduce(cnt[:], compare_fan, AX.X, ALU.add), dve)
            link(v.tensor_scalar(cnt[:], cnt[:], -1.0, 0.0, ALU.add, ALU.max), dve)
            link(v.scalar_tensor_tensor(row[:], row[:], float(FAN), cnt[:], ALU.mult, ALU.add), dve)
            v.tensor_scalar(start_i[:], row[:], float(LAST_START), None, ALU.min).then_inc(s["starts_found"], 1)

            dve.wait_ge(s["x_loaded"], 32)
            sq = parts[:].rearrange("p k c -> p (k c)").bitcast(F32).rearrange("p (k d) -> p k d", d=D)
            mean, var, inv, tmp = (stat[:, j, :] for j in range(4))

            def wide(a):
                return a.unsqueeze(2).to_broadcast([P, KT, D])

            link(v.tensor_reduce(mean, msg[:], AX.X, ALU.add), dve)
            link(v.tensor_scalar(mean, mean, LN_SUM_TO_MEAN, None, ALU.mult), dve)
            v.tensor_tensor(msg[:], msg[:], wide(mean), ALU.subtract).then_inc(s["x_centred"], 1)
            dve.wait_ge(s["squares_made"], 1)
            link(v.tensor_reduce(var, sq, AX.X, ALU.add), dve)
            v.tensor_scalar(var, var, LN_SUM_TO_MEAN, EPS, ALU.mult, ALU.add).then_inc(s["variance_made"], 1)
            dve.wait_ge(s["root_made"], 1)
            link(v.reciprocal(inv, inv), dve)
            link(v.tensor_tensor(tmp, inv, inv, ALU.mult), dve)
            link(v.tensor_tensor(tmp, tmp, var, ALU.mult), dve)
            link(v.tensor_scalar(tmp, tmp, -0.5, 1.5, ALU.mult, ALU.add), dve)
            link(v.tensor_tensor(inv, inv, tmp, ALU.mult), dve)
            for w in range(2):
                t = slice(w * HALF_T, (w + 1) * HALF_T)
                v.scalar_tensor_tensor(stacked_h0[:, :, w, :], msg[:, t, :], 0.0,
                                       inv[:, t].unsqueeze(2).to_broadcast([P, HALF_T, D]), ALU.max,
                                       ALU.mult).then_inc(s["h0_made"], 1)

            def make_keys(n):
                t = slice(n * KG, (n + 1) * KG)
                dve.wait_ge(windows_gathered[n], 16 * KG)
                link(v.tensor_scalar(win_row, win[:, t, :], LO_BITS, None, ALU.arith_shift_right), dve)
                link(v.tensor_scalar(win[:, t, :], win[:, t, :], (1 << LO_BITS) - 1, None, ALU.bitwise_and), dve)
                v.tensor_scalar(weight[:, t, 0:WIN], win[:, t, :], float(1 << (LO_BITS - 1)), NIBBLE - 1.0, ALU.is_ge,
                                ALU.mult)
                link(v.tensor_tensor(win_rowf, win_row,
                                     node_hi[:, t].unsqueeze(2).to_broadcast([P, KG, WIN]), ALU.subtract), dve)
                v.tensor_scalar(win[:, t, :], win[:, t, :], (1 << (LO_BITS - 1)) - 1, None, ALU.bitwise_and).then_inc(
                    s["columns_found"], 1)
                link(v.tensor_scalar(weight[:, t, 0:WIN], weight[:, t, 0:WIN], 1.0, None, ALU.add), dve)
                link(v.tensor_scalar(row_key[:, t, 0:WIN], win_rowf, float(P), -1.0, ALU.min, ALU.max), dve)
                v.tensor_copy(row_key[:, t, WIN:2 * P], row_key[:, t, MAIN:WIN])
                v.tensor_copy(weight[:, t, WIN:2 * P], weight[:, t, MAIN:WIN]).then_inc(s["keys_made"], 1)

            def keep_overs(n):
                dve.wait_ge(s["keys_turned"], n + 1)
                over = key_bank(n)[:, 1, :, :].rearrange("p j (b pair two) -> p j b pair two", pair=WAVE, two=2)
                to = key_rows(n)[:, :, :, MAINS:WKEYS]
                v.tensor_copy(to[0:OVER], over[0:OVER, :, :, :, 0])
                v.tensor_copy(to[OVER:P], over[OVER:P, :, :, :, 1]).then_inc(s["overs_kept"], 1)

            for n in range(WT // KG):
                make_keys(n)
                for m in range((n - 1) * KG if n else 0, n * KG):
                    keep_overs(m)
            for m in range(WT - KG, WT):
                keep_overs(m)
            dve.wait_ge(s["overs_kept"], WT)

            def hot_tile(i, first):
                def compare_keys(out, width, key):
                    v_shape = [P, WKEYS, width // 2, 2]
                    return v.tensor_tensor(
                        out.rearrange("p c (m two) -> p c m two", two=2),
                        iota[:, 0:width].rearrange("p (m two) -> p m two", two=2).unsqueeze(1).to_broadcast(v_shape),
                        key.unsqueeze(2).to_broadcast(v_shape), ALU.is_equal)

                v_shape = [P, MAINS, P // 2, 2]
                for q in range(IW):
                    u, slot = q // TW, q % HOTS
                    if q % TW == 0:
                        dve.wait_ge(s["keys_copied"], i * 2 + u + 1)
                    if not first or q >= HOTS:
                        dve.wait_ge(s["batch_multiplied"], i * IB + (q - HOTS + 1) * WB)
                    k = [(n * TW + q % TW) * WKEYS for n in range(KINDS)]
                    compare_keys(hot_r[:, slot, :, :], P, key_now[:, u, k[0]:k[0] + WKEYS, :]).then_inc(s["rows_made"], 1)
                    compare_keys(hot_c[:, slot, :, 0:LO], LO, key_now[:, u, k[1]:k[1] + WKEYS, :])
                    dve.wait_ge(s["rows_made"], i * IW + q + 1)
                    rows = hot_r[:, slot, 0:MAINS, :].rearrange("p c (m two) -> p c m two", two=2)
                    v.tensor_tensor(rows, rows, key_now[:, u, k[2]:k[2] + MAINS, :].unsqueeze(2).to_broadcast(v_shape),
                                    ALU.mult).then_inc(s["hots_made"], 1)
                    if q == 5:
                        dve.wait_ge(s["message0_done"], i + 1)
                        v.tensor_tensor(halves[:, ds(i, 1), :, :],
                                        ps[:, 7, 0:P].rearrange("p (a w d) -> p a w d", a=1, w=2),
                                        b2row[:, 0:1, :].unsqueeze(1).to_broadcast([P, 1, 2, D]), ALU.add).then_inc(
                            s["message_kept"], 1)
                    if q == 6:
                        dve.wait_ge(s["message_kept"], i + 1)
                        v.tensor_reduce(peak[:, ds(i, 1)], halves[:, ds(i, 1), :, :].rearrange("p a w d -> p (a w) d"),
                                        AX.XY, ALU.max, apply_absolute_value=True).then_inc(s["peak_found"], 1)

            hot_tile(0, True)
            with dve.Fori(1, BUILD) as i:
                hot_tile(i, False)

            def judge():
                v.tensor_reduce(good[:, 0:1], row_edges, AX.XY, ALU.add)
                link(v.tensor_reduce(good[:, 1:2], row_edges, AX.XY, ALU.max), dve)
                link(v.tensor_scalar(good[:, 1:2], good[:, 1:2], NIBBLE - 1.0, None, ALU.is_le), dve)

            def find_peak(l, found, peaks):
                dve.wait_ge(s["peak_found"], found)
                v.tensor_reduce(scal[:, l, 0:1], peak[:, 0:peaks], AX.X, ALU.max).then_inc(s["peak_made"], 1)

            def make_scale(l):
                c = [scal[:, l, j:j + 1] for j in range(8)]
                dve.wait_ge(s["peak_shared"], l + 1)
                link(v.tensor_scalar(c[2], c[1], 2.0 ** -100, None, ALU.max), dve)
                link(v.tensor_scalar(c[3].bitcast(I32), c[2].bitcast(I32), 0x7F800000, None, ALU.bitwise_and), dve)
                link(v.reciprocal(c[4], c[3]), dve)
                link(v.tensor_scalar(c[6], c[3], 1.0 / SCALED / COUNT_UNIT, None, ALU.mult), dve)
                v.tensor_scalar(c[5], c[4], SCALED, None, ALU.mult).then_inc(s["scale_made"], 1)

            def lower_parts(l, n):
                t = slice(ORDER[n] * CK, (ORDER[n] + 1) * CK)
                dve.wait_ge(s["scale_made"], l + 1)
                dve.wait_ge(s["upper_made"], l * CH + n + 1)
                v.scalar_tensor_tensor(parts[:, t, D:P], msg[:, t, :], scal[:, l, 5:6], parts[:, t, 0:D], ALU.mult,
                                       ALU.subtract).then_inc(s["parts_made"], 1)

            def check_scale(l):
                dve.wait_ge(s["peak_found"], BUILD + l * 2 * SB)
                link(v.tensor_reduce(fits[:, l, 0:1], peak[:, EARLY_PEAKS:2 * SB], AX.X, ALU.max), dve)
                link(v.tensor_scalar(fits[:, l, 1:2], fits[:, l, 0:1], scal[:, l, 5:6], SCALED_LIMIT, ALU.mult, ALU.is_le), dve)

            def unpack(sbase, l, c, after):
                g = sbase + l * SB + after
                dve.wait_ge(counts_loaded[c % RING], (g * SLOT_LOADS[c % RING] + c // RING + 1) * 16)
                if c >= WIDE:
                    dve.wait_ge(s["counts_used"], g * (CH - 1) + c - WIDE + 1)
                elif not (isinstance(g, int) and g == 0):
                    if c == WIDE - 1:
                        dve.wait_ge(s["sums_done"], g * SBB)
                    else:
                        dve.wait_ge(s["counts_used"], g * (CH - 1))
                packed = ring[:, c % RING, :].bitcast(U16)
                v.tensor_scalar(spread[:, c % WIDE, 0, :].bitcast(U16), packed, 0x0F0F, None, ALU.bitwise_and)
                v.tensor_scalar(spread[:, c % WIDE, 1, :].bitcast(U16), packed, 4, 0x0F0F, ALU.logical_shift_right,
                                ALU.bitwise_and).then_inc(s["counts_unpacked"], 1)

            def read_sums(l, i):
                g = i + l * SB
                for b in range(SBB):
                    dve.wait_ge(s["sums_done"], g * SBB + b + 1)
                    if l and b == 0:
                        dve.wait_ge(s["h_saved"], l * SB)
                    cols = slice(b * NB, (b + 1) * NB)
                    own = slice(b // 2 * D, b // 2 * D + D)
                    other = slice(D - b // 2 * D, P - b // 2 * D)
                    v.tensor_scalar(zP[other, cols], ps[other, b, 0:NB], scal[other, l, 6:7], None, ALU.mult)
                    v.scalar_tensor_tensor(zP[own, cols], ps[own, b, 0:NB], scal[own, l, 6:7],
                                           hT[own, ds(i * SBH + b % 2 * NB, NB)], ALU.mult,
                                           ALU.add).then_inc(s["sums_read"], 1)

            def finish(l, i, w):
                g = i + l * SB
                first, n = FINISH[w]
                bank = ps[:, 6 + w, 0:n * P].rearrange("p (k w d) -> p k w d", w=2, d=D)
                dve.wait_ge(s["m_done"], g * 2 + w + 1)
                if l < L - 1:
                    to = halves[:, ds(i * 7 + first, n), :, :]
                    v.tensor_tensor(to, bank, b2row[:, l + 1:l + 2, :].unsqueeze(1).to_broadcast([P, n, 2, D]),
                                    ALU.add).then_inc(s["m_kept"], 1)
                    dve.wait_ge(s["m_kept"], g * 2 + w + 1)
                    v.tensor_reduce(peak[:, ds(i * 2 + w, 1)], to, AX.XYZ, ALU.max,
                                    apply_absolute_value=True).then_inc(s["peak_found"], 1)
                else:
                    to, old = (a.rearrange("p (w k) d -> p k w d", w=2)[:, first:first + n, :, :] for a in (out_t, x_t))
                    if w == 0 and not (isinstance(i, int) and i == 0):
                        dve.wait_ge(s["out_stored"], 32 * i)
                    v.tensor_tensor(to, bank, bfrow[:].unsqueeze(1).unsqueeze(1).to_broadcast([P, n, 2, D]),
                                    ALU.add).then_inc(s["m_kept"], 1)
                    dve.wait_ge(s["m_kept"], g * 2 + w + 1)
                    dve.wait_ge(s["x_again"], 32 * i + (48 if isinstance(i, int) and i == SB - 1 else 32))
                    v.tensor_tensor(to, to, old, ALU.add).then_inc(s["out_made"], 1)

            def stretch(l, i, before, last=False):
                if before:
                    read_sums(*before)
                for c in range(1, CH):
                    unpack(i, l, c, 0)
                    if c in (8, 9) and before:
                        finish(*before, c - 8)
                        if last and c == 9 and l < L - 1:
                            find_peak(l + 1, BUILD + l * 2 * SB + EARLY_PEAKS, EARLY_PEAKS)
                        if before[0] < l and c == 9:
                            lower_parts(l, EARLY)
                            lower_parts(l, EARLY + 1)
                            check_scale(l)
                    if last and l < L - 1 and c >= 11:
                        if c == 11:
                            make_scale(l + 1)
                        for n in range(4 * (c - 11), min(4 * (c - 10), EARLY - 1)):
                            lower_parts(l + 1, n)
                if not (last and l == L - 1):
                    unpack(i, l, 0, 1)
                if last and l < L - 1:
                    lower_parts(l + 1, EARLY - 1)

            dve.wait_ge(counts_stored[0], 16 * BUILD)
            dve.wait_ge(counts_stored[1], 16 * BUILD)
            dve.wait_ge(s["keys_copied"], 2 * (BUILD + 1))
            dve.wait_ge(s["overs_copied"], 2 * (BUILD + 1))
            find_peak(0, BUILD, BUILD)
            unpack(0, 0, 0, 0)
            make_scale(0)
            for n in range(CH):
                lower_parts(0, n)
            for l in range(L):
                stretch(l, 0, (l - 1, SB - 1) if l else None)
                if l == 0:
                    judge()
                with dve.Fori(1, SB - 1) as i:
                    stretch(l, i, (l, i - 1))
                stretch(l, SB - 1, (l, SB - 2), True)
            link(v.tensor_tensor(good[:, 1:2], good[:, 1:2], fits[:, 1, 1:2], ALU.mult), dve)
            v.tensor_tensor(good[:, 1:2], good[:, 1:2], fits[:, 2, 1:2], ALU.mult).then_inc(s["good_made"], 1)
            read_sums(L - 1, SB - 1)
            finish(L - 1, SB - 1, 0)
            finish(L - 1, SB - 1, 1)
            dve.wait_ge(s["good_shared"], 1)
            link(v.tensor_scalar(good[:, 2:3], good[:, 2:3], float(E), None, ALU.is_equal), dve)
            link(v.tensor_scalar(good[:, 3:4], good[:, 3:4], float(P), None, ALU.is_equal), dve)
            v.tensor_tensor(good_i[:], good[0:1, 2:3], good[0:1, 3:4], ALU.mult).then_inc(s["verdict"], 1)

            def tile(l, i):
                if l == -1 and isinstance(i, int):
                    v.memset(msg[:], 0.0).then_inc(gs["zeros_made"], 1)
                pe_before = tiles_before("tensor", l, i)
                dve.wait_ge(gs["loaded"], tiles_before("loaded", l, i) + TILE_SIGNALS["loaded"][l + 1])
                if l == -1:
                    v.tensor_copy(tile_z, tile_h).then_inc(gs["vector"], 1)
                else:
                    v.tensor_tensor(tile_z, tile_h, tile_agg, ALU.add).then_inc(gs["vector"], 1)
                if 0 <= l < L - 1:
                    dve.wait_ge(gs["tensor"], pe_before + 4)
                    v.tensor_tensor(tile_hn, ps[:, 3, 0:D], b2row[:, l, :], ALU.add).then_inc(gs["vector"], 1)
                dve.wait_ge(gs["tensor"], pe_before + TILE_SIGNALS["tensor"][l + 1])
                if l < L - 1:
                    v.tensor_tensor(tile_m, ps[:, 5, 0:D], b2row[:, l + 1, :], ALU.add).then_inc(gs["vector"], 1)
                else:
                    n = TAIL if isinstance(i, int) else P
                    v.tensor_tensor(tile_m[0:n], ps[0:n, 5, 0:D], bfrow[0:n], ALU.add).then_inc(gs["vector"], 1)
                    dve.wait_ge(gs["vector"], tiles_before("vector", l, i) + 2)
                    v.tensor_tensor(tile_m[0:n], tile_m[0:n], tile_x[0:n], ALU.add).then_inc(gs["vector"], 1)

            def edges(l):
                with dve.Fori(0, EDGE_CHUNKS) as c:
                    dve.wait_ge(es[l]["src_loaded"], c * 16 + 16)
                    v.tensor_copy(e_srcf, e_src).then_inc(es[l]["vector"], 1)
                    dve.wait_ge(es[l]["vector"], c * 7 + 1)
                    v.tensor_scalar(e_diag, ident[:], e_srcf, None, ALU.mult).then_inc(es[l]["vector"], 1)
                    dve.wait_ge(es[l]["tensor"], c * 2 + 1)
                    v.tensor_scalar(e_same, ps[:, 6, 0:P], e_srcf, None, ALU.is_equal).then_inc(es[l]["vector"], 1)
                    dve.wait_ge(es[l]["vector"], c * 7 + 3)
                    dve.wait_ge(gs["below_made"], 1)
                    v.tensor_tensor(e_before, e_same, below, ALU.mult).then_inc(es[l]["vector"], 1)
                    dve.wait_ge(es[l]["vector"], c * 7 + 4)
                    v.tensor_reduce(e_seen, e_before, AX.X, ALU.add).then_inc(es[l]["vector"], 1)
                    dve.wait_ge(es[l]["vector"], c * 7 + 5)
                    v.scalar_tensor_tensor(e_to, e_seen, 65536.0, e_srcf, ALU.mult, ALU.add).then_inc(
                        es[l]["vector"], 1)
                    dve.wait_ge(es[l]["tensor"], c * 2 + 2)
                    dve.wait_ge(es[l]["sums"], c * 16 + 16)
                    v.tensor_tensor(e_agg, e_agg, ps[:, 7, 0:D], ALU.add).then_inc(es[l]["vector"], 1)

            general(dve, tile, edges)

        @block.scalar
        def _(act):
            a = nc.scalar
            act.wait_ge(s["src_loaded"], 16)
            a.activation(pa, src_t, ACT.Copy, scale=1.0 / LO, bias=-0.5 + 1.0 / 1024).then_inc(s["quotients_made"], 1)
            act.wait_ge(s["x_centred"], 1)
            a.activation(parts[:].rearrange("p k c -> p (k c)").bitcast(F32).rearrange("p (k d) -> p k d", d=D), msg[:],
                         ACT.Square).then_inc(s["squares_made"], 1)
            act.wait_ge(s["variance_made"], 1)
            a.activation(stat[:, 2, :], stat[:, 1, :], ACT.Sqrt).then_inc(s["root_made"], 1)

            def keep_mains(n):
                act.wait_ge(s["keys_turned"], n + 1)
                a.copy(key_rows(n)[:, :, :, 0:MAINS],
                       key_bank(n)[:, 0, :, :].rearrange("p j (b c) -> p j b c", c=MAINS)).then_inc(s["mains_kept"], 1)

            for n in range(TURNS):
                w = min(4, HALF_T - 4 * n) * P
                act.wait_ge(s["h0_turned"], n + 1)
                a.copy(hT[:, n * 4 * P:n * 4 * P + w], ps[:, 2 + n % 2, 0:w]).then_inc(s["h0_kept"], 1)
            for m in range(WT // KG):
                t = slice(m * KG, (m + 1) * KG)
                act.wait_ge(s["columns_found"], m + 1)
                a.copy(col_key[:, t, 0:WIN], win[:, t, :])
                a.copy(col_key[:, t, WIN:2 * P], win[:, t, MAIN:WIN]).then_inc(s["columns_kept"], 1)
                for n in range((m - 1) * KG if m else 0, m * KG):
                    keep_mains(n)
            for n in range(WT - KG, WT):
                keep_mains(n)

            act.wait_ge(s["weights_loaded"], 16 * WEIGHT_LOADS)

            def weight_overs(i, q):
                slot = q // WB % HOTS
                if q % TB == 0:
                    wait_alone(act, s["overs_copied"], i * 2 + q // TB + 1)
                if q % WB == 0:
                    wait_alone(act, s["rows_made"], i * IW + q // WB + 1)
                for n in range(q % WB * BATCH, (q % WB + 1) * BATCH):
                    rows = hot_r[:, slot, MAINS + n, :]
                    last = a.activation(rows, rows, ACT.Copy, scale=over_weight[:, q // TB, q // WB % TW, n:n + 1])
                last.then_inc(s["overs_weighted"], 1)

            def keep_batch(i, q, first):
                slot = q % PSLOTS
                if q % TB == 0 and not first:
                    act.wait_ge(counts_stored[q // TB], i * 16)
                wait_alone(act, s["batch_multiplied"], i * IB + q + 1)
                g = q * 2 * BATCH
                banks = ps[:, 2 * slot:2 * slot + 2, 0:BATCH * WITH].rearrange("p k (pair n) -> p k pair n", n=WITH)
                a.activation(stage[:, g:g + 2 * BATCH, :].rearrange("p (pair k) n -> p k pair n", k=2),
                             banks[:, :, :, 0:LO], ACT.Copy)
                a.activation(row_edges[:, ds(i * IB + q, 1), :].rearrange("p a (pair k) -> p k (a pair)", k=2),
                             banks[:, :, :, LO], ACT.Copy).then_inc(s["batch_kept"], 1)

            def keep_tile(i, first):
                for q in range(IB):
                    weight_overs(i, q)
                    if q >= KEEP_LAG:
                        keep_batch(i, q - KEEP_LAG, first)
                    elif not first:
                        keep_batch(i - 1, IB + q - KEEP_LAG, True)
                    if q == 3:
                        act.wait_ge(s["hidden0_done"], i + 1)
                        if not first:
                            act.wait_ge(s["message0_done"], i)
                        a.activation(uS[:], ps[:, 6, 0:P], ACT.Relu, bias=b1s[:, 0:1]).then_inc(
                            s["hidden0_kept"], 1)

            keep_tile(0, True)
            with act.Fori(1, BUILD) as i:
                keep_tile(i, False)
            for q in range(IB - KEEP_LAG, IB):
                keep_batch(BUILD - 1, q, True)

            def epilogue(l, i):
                g = i + l * SB
                for b in range(2):
                    act.wait_ge(s["u_done"], g * 2 + b + 1)
                    a.activation(U[:, b * NB:(b + 1) * NB], ps[:, 4 + b, 0:NB], ACT.Relu,
                                 bias=b1s[:, l:l + 1]).then_inc(s["u_kept"], 1)
                for b in range(2):
                    act.wait_ge(s["h_done"], g * 2 + b + 1)
                    if b == 0 and l < L - 1 and not (isinstance(i, int) and g == 0):
                        act.wait_ge(s["h_saved"], g)
                    if b == 0 and l == L - 1:
                        act.wait_ge(s["h_saved"], (L - 1) * SB)
                    a.activation(hN[:, b * NB:(b + 1) * NB], ps[:, 4 + b, 0:NB], ACT.Identity,
                                 bias=b2s[:, l:l + 1]).then_inc(s["h_kept"], 1)
                for b in range(2 if l < L - 1 else 0):
                    act.wait_ge(s["v_done"], g * 2 + b + 1)
                    a.activation(V[:, b * NB:(b + 1) * NB], ps[:, 4 + b, 0:NB], ACT.Relu,
                                 bias=b1s[:, l + 1:l + 2]).then_inc(s["v_kept"], 1)

            def upper_parts(l, n):
                t = slice(ORDER[n] * CK, (ORDER[n] + 1) * CK)
                if l:
                    last = l * SB - 1
                    if n < CH - 1:
                        act.wait_ge(s["counts_used"], last * (CH - 1) + n + 1)
                    else:
                        act.wait_ge(s["sums_done"], (last + 1) * SBB)
                    if n >= EARLY:
                        act.wait_ge(s["m_kept"], last * 2 + 2)
                a.activation(parts[:, t, 0:D], msg[:, t, :], ACT.Copy, scale=scal[:, l, 5:6]).then_inc(s["upper_made"], 1)

            act.wait_ge(s["message_kept"], BUILD)
            act.wait_ge(s["scale_made"], 1)
            act.wait_ge(s["h0_stored"], 32)
            for n in range(CH):
                upper_parts(0, n)
            for l in range(L):
                epilogue(l, 0)
                with act.Fori(1, SB - 1) as i:
                    epilogue(l, i)
                if l < L - 1:
                    act.wait_ge(s["scale_made"], l + 2)
                    for n in range(EARLY):
                        upper_parts(l + 1, n)
                epilogue(l, SB - 1)
                if l < L - 1:
                    for n in range(EARLY, CH):
                        upper_parts(l + 1, n)

            def tile(l, i):
                pe_before = tiles_before("tensor", l, i)
                relu, plain = ACT.Relu, ACT.Identity
                act.wait_ge(gs["tensor"], pe_before + 1)
                a.copy(zT_g, ps[0:D, 0, 0:P]).then_inc(gs["scalar"], 1)
                if l >= 0:
                    act.wait_ge(gs["tensor"], pe_before + 2)
                    a.activation(uT_g, ps[0:D, 1, 0:P], relu, bias=b1s[0:D, l:l + 1]).then_inc(gs["scalar"], 1)
                    act.wait_ge(gs["tensor"], pe_before + 3)
                    a.activation(hT_g, ps[0:D, 2, 0:P], plain, bias=b2s[0:D, l:l + 1]).then_inc(gs["scalar"], 1)
                if l < L - 1:
                    act.wait_ge(gs["tensor"], pe_before + (2 if l == -1 else 5))
                    a.activation(vT_g, ps[0:D, 4, 0:P], relu, bias=b1s[0:D, l + 1:l + 2]).then_inc(gs["scalar"], 1)

            general(act, tile, None)

        @block.tensor
        def _(pe):
            t = nc.tensor
            pe.wait_ge(s["constants_made"], 6)
            pe.wait_ge(s["tops_cast"], 1)
            t.matmul(ps[:, 0, 0:TOP], ones[0:1, :], first_f, start=True, stop=True).then_inc(s["tops_spread"], 1)
            pe.wait_ge(s["h0_made"], 2)
            def turn_keys(n):
                pe.wait_ge(s["keys_made"], n // KG + 1)
                pe.wait_ge(s["columns_kept"], n // KG + 1)
                if n >= 3:
                    pe.wait_ge(s["mains_kept"], n - 2)
                    pe.wait_ge(s["overs_kept"], n - 2)
                for j, key in enumerate((row_key, col_key, weight)):
                    for k in range(2):
                        last = t.transpose(key_bank(n)[:, k, j, :], key[:, n, k * P:(k + 1) * P], ident16[:])
                last.then_inc(s["keys_turned"], 1)

            for n in range(TURNS):
                if n >= 2:
                    pe.wait_ge(s["h0_kept"], n - 1)
                for j in range(min(4, HALF_T - 4 * n)):
                    last = t.transpose(ps[:, 2 + n % 2, j * P:(j + 1) * P],
                                       stacked_h0[:, 4 * n + j, :, :].rearrange("p w d -> p (w d)"), ident[:])
                last.then_inc(s["h0_turned"], 1)
            for n in range(WT):
                turn_keys(n)

            pe.wait_ge(s["weights_loaded"], 16 * WEIGHT_LOADS)
            pe.wait_ge(s["h0_kept"], TURNS)
            pe.wait_ge(s["mains_kept"], WT)
            pe.wait_ge(s["overs_kept"], WT)

            def multiply_tile(i, first):
                for q in range(IB):
                    hot, slot = q // WB % HOTS, q % PSLOTS
                    if q % WB == 0:
                        wait_alone(pe, s["hots_made"], i * IW + q // WB + 1)
                        wait_alone(pe, s["inverses_made"], i * IW + q // WB + 1)
                    wait_alone(pe, s["overs_weighted"], i * IB + q + 1)
                    if q >= PSLOTS:
                        wait_alone(pe, s["batch_kept"], i * IB + q - PSLOTS + 1)
                    elif not first:
                        before = max(k for k in range(IB) if k % PSLOTS == slot)
                        wait_alone(pe, s["batch_kept"], i * IB + before + 1 - IB)
                    for n in range(2 * BATCH):
                        pair, k = n // 2, n % 2
                        half = slice(k * OVER, (k + 1) * OVER)
                        main, over = q % WB * 2 * BATCH + n, MAINS + q % WB * BATCH + pair
                        prod = ps[:, 2 * slot + k, pair * WITH:pair * WITH + LO + 1]
                        t.matmul(prod, hot_r[:, hot, main, :], hot_c[:, hot, main, 0:LO + 1], start=True, stop=False)
                        last = t.matmul(prod, hot_r[half, hot, over, :], hot_c[half, hot, over, 0:LO + 1], start=False,
                                        stop=True)
                    last.then_inc(s["batch_multiplied"], 1)
                    if q == 1:
                        wait_alone(pe, s["h_copied"], i + 1)
                        if not first:
                            wait_alone(pe, s["hidden0_kept"], i)
                        t.matmul(ps[:, 6, 0:P], W1b[:, 0, :], hS[:], start=True, stop=True).then_inc(
                            s["hidden0_done"], 1)
                    if q == 4:
                        wait_alone(pe, s["hidden0_kept"], i + 1)
                        if not first:
                            wait_alone(pe, s["message_kept"], i)
                        t.matmul(ps[:, 7, 0:P], uS[:], W2b[:, 0, :], start=True, stop=True).then_inc(
                            s["message0_done"], 1)

            multiply_tile(0, True)
            with pe.Fori(1, BUILD) as i:
                multiply_tile(i, False)

            def mlp_stage(l, i, n):
                g = i + l * SB
                final = l == L - 1
                steps = ["u0", "u1", "h", "v", "m0", "m1"] if not final else ["u0", "u1", "h", "", "m0", "m1"]
                if n >= len(steps) or not steps[n]:
                    return
                kind = steps[n][0]
                if kind == "u":
                    b = int(steps[n][1])
                    wait_alone(pe, s["sums_read"], g * SBB + b + 3)
                    for w in range(2):
                        cols = slice((2 * w + b) * NB, (2 * w + b + 1) * NB)
                        last = t.matmul(ps[w * D:(w + 1) * D, 4 + b, 0:NB], W1s[:, l, :], zP[:, cols], start=True, stop=True)
                    last.then_inc(s["u_done"], 1)
                elif kind in "hv":
                    frm, w, ready, done = {"h": (U, W2b[:, l, :], "u_kept", "h_done"),
                                           "v": (hN, None if final else W1b[:, l + 1, :], "h_kept", "v_done")}[kind]
                    for b in range(2):
                        wait_alone(pe, s[ready], g * 2 + b + 1)
                        t.matmul(ps[:, 4 + b, 0:NB], w, frm[:, b * NB:(b + 1) * NB], start=True, stop=True).then_inc(
                            s[done], 1)
                else:
                    w = int(steps[n][1])
                    if final:
                        frm, weights = hN, Wfb[:]
                        pe.wait_ge(s["h_kept"], (g + 1) * 2)
                    else:
                        frm, weights = V, W2b[:, l + 1, :]
                        pe.wait_ge(s["v_kept"], (g + 1) * 2)
                    first, tiles = FINISH[w]
                    for k in range(tiles):
                        c = (first + k) * P
                        last = t.matmul(ps[:, 6 + w, k * P:(k + 1) * P], frm[:, c:c + P], weights, start=True, stop=True)
                    last.then_inc(s["m_done"], 1)

            def multiply_stretch(l, i, before):
                g = i + l * SB
                for c in range(CH):
                    wait_alone(pe, s["counts_unpacked"], g * CH + c + 1)
                    if isinstance(i, int):
                        pe.wait_ge(s["parts_made"], l * CH + c + 1)
                    steps = [(k, b) for k in range(CK) for b in range(SBB)]
                    if c in (0, CH - 1):
                        steps.sort(key=lambda step: step[1])
                    for k, b in steps:
                        start, stop = c == 0 and k == 0, c == CH - 1 and k == CK - 1
                        if start and not (isinstance(i, int) and g == 0):
                            wait_alone(pe, s["sums_read"], g * SBB + b + 1 - SBB)
                        at = k * SBH + b % 2 * NB
                        last = t.matmul(ps[:, b, 0:NB], parts[:, ORDER[c] * CK + k, :],
                                        spread[:, c % WIDE, b // 2, at:at + NB].bitcast(F8), start=start, stop=stop)
                        if stop:
                            last.then_inc(s["sums_done"], 1)
                    if c < CH - 1:
                        last.then_inc(s["counts_used"], 1)
                    if before:
                        mlp_stage(*before, c)

            for l in range(L):
                multiply_stretch(l, 0, (l - 1, SB - 1) if l else None)
                with pe.Fori(1, SB) as i:
                    multiply_stretch(l, i, (l, i - 1))
            for n in range(8):
                mlp_stage(L - 1, SB - 1, n)

            def tile(l, i):
                act_before = tiles_before("scalar", l, i)
                wait_alone(pe, gs["vector"], tiles_before("vector", l, i) + 1)
                t.transpose(ps[0:D, 0, 0:P], tile_z, ident[:]).then_inc(gs["tensor"], 1)
                wait_alone(pe, gs["scalar"], act_before + 1)
                h = zT_g
                if l >= 0:
                    t.matmul(ps[0:D, 1, 0:P], W1s[0:D, l, :], zT_g, start=True, stop=True).then_inc(gs["tensor"], 1)
                    wait_alone(pe, gs["scalar"], act_before + 2)
                    t.matmul(ps[0:D, 2, 0:P], W2s[:, l, :], uT_g, start=True, stop=True).then_inc(gs["tensor"], 1)
                    if l < L - 1:
                        t.matmul(ps[:, 3, 0:D], uT_g, W2s[:, l, :], start=True, stop=True).then_inc(gs["tensor"], 1)
                    wait_alone(pe, gs["scalar"], act_before + 3)
                    h = hT_g
                if l < L - 1:
                    t.matmul(ps[0:D, 4, 0:P], W1s[0:D, l + 1, :], h, start=True, stop=True).then_inc(gs["tensor"], 1)
                    wait_alone(pe, gs["scalar"], act_before + TILE_SIGNALS["scalar"][l + 1])
                    t.matmul(ps[:, 5, 0:D], vT_g, W2s[:, l + 1, :], start=True, stop=True).then_inc(gs["tensor"], 1)
                else:
                    t.matmul(ps[:, 5, 0:D], h, Wfs[:], start=True, stop=True).then_inc(gs["tensor"], 1)

            def edges(l):
                with pe.Fori(0, EDGE_CHUNKS) as c:
                    wait_alone(pe, es[l]["vector"], c * 7 + 2)
                    t.matmul(ps[:, 6, 0:P], ones[:], e_diag, start=True, stop=True).then_inc(es[l]["tensor"], 1)
                    wait_alone(pe, es[l]["vector"], c * 7 + 3)
                    wait_alone(pe, es[l]["messages"], c * 16 + 16)
                    t.matmul(ps[:, 7, 0:D], e_same, e_msg, start=True, stop=True).then_inc(es[l]["tensor"], 1)

            general(pe, tile, edges)


_INS = ["x", "src", "dst", "L0_gnn_W1", "L0_gnn_b1", "L0_gnn_W2", "L0_gnn_b2", "L0_gnn_Wf", "L0_gnn_bf"]


def kernel(**inputs):
    import numpy as _np
    import concourse.bacc as _bacc
    from concourse import mybir as _mybir
    from concourse.bass_utils import run_bass_kernel_spmd as _run

    nc = _bacc.Bacc("TRN2", target_bir_lowering=False, num_devices=1)
    arrays, args = {}, []
    for name in _INS:
        a = _np.ascontiguousarray(inputs[name])
        arrays[f"in_{name}_dram"] = a
        args.append(nc.dram_tensor(f"in_{name}_dram", a.shape, _mybir.dt.from_np(a.dtype), kind="ExternalInput").ap())
    args.append(nc.dram_tensor("out_dram", (N, D), _mybir.dt.float32, kind="ExternalOutput").ap())
    gnn_kernel(nc, *args)
    r = _run(nc, [arrays], core_ids=[0])
    return r.results[0]["out_dram"]
```
